# Optimizing a Trainium2 kernel written in Bass

```python
import numpy as np
import jax
import jax.numpy as jnp

def _softmax(x, axis=-1):
    return jax.nn.softmax(x, axis=axis)

def _gelu(x):
    return jax.nn.gelu(x, approximate=True)

def _silu(x):
    return jax.nn.silu(x)

def _sigmoid(x):
    return jax.nn.sigmoid(x)

def _layernorm(x, axis=-1, eps=1e-05):
    m = jnp.mean(x, axis=axis, keepdims=True)
    v = jnp.var(x, axis=axis, keepdims=True)
    return (x - m) / jnp.sqrt(v + eps)

def _scatter_add(tgt, idx, src, axis=0):
    return tgt.at[idx].add(src)

def _segment_sum(src, seg, n):
    return jax.ops.segment_sum(src, seg, n)
kernel_name = 'mk_dlrm_tower_d1_rec_r8_b148cd'

def setup_inputs(seed: int=0):
    np.random.seed(seed)
    _w = jnp.asarray

    def _rec_inputs():
        import jax
        import jax.numpy as jnp
        _tk = jax.random.key(seed)
        dense_ctx = jax.random.normal(jax.random.fold_in(_tk, 190), (2048, 16), jnp.float32)
        ids = jnp.stack([jax.random.randint(jax.random.fold_in(_tk, 200 + f), (2048,), 0, v, jnp.int32) for f, v in enumerate([1000, 125000, 1250, 12500, 125000, 1000, 1000, 125000, 1250, 1250, 125000, 125000, 1000, 12500, 1250, 12500, 1000, 1000, 125000, 1000, 125000, 1250, 12500, 1250, 125000, 1000, 12500, 12500, 1000, 12500, 12500, 1000, 125000, 125000, 1000, 12500, 12500, 12500, 1000])], axis=1)
        tbl_0 = 0.05 * jax.random.normal(jax.random.fold_in(_tk, 500 + 0), (1000, 16), jnp.float32)
        tbl_1 = 0.05 * jax.random.normal(jax.random.fold_in(_tk, 500 + 1), (125000, 16), jnp.float32)
        tbl_2 = 0.05 * jax.random.normal(jax.random.fold_in(_tk, 500 + 2), (1250, 16), jnp.float32)
        tbl_3 = 0.05 * jax.random.normal(jax.random.fold_in(_tk, 500 + 3), (12500, 16), jnp.float32)
        tbl_4 = 0.05 * jax.random.normal(jax.random.fold_in(_tk, 500 + 4), (125000, 16), jnp.float32)
        tbl_5 = 0.05 * jax.random.normal(jax.random.fold_in(_tk, 500 + 5), (1000, 16), jnp.float32)
        tbl_6 = 0.05 * jax.random.normal(jax.random.fold_in(_tk, 500 + 6), (1000, 16), jnp.float32)
        tbl_7 = 0.05 * jax.random.normal(jax.random.fold_in(_tk, 500 + 7), (125000, 16), jnp.float32)
        tbl_8 = 0.05 * jax.random.normal(jax.random.fold_in(_tk, 500 + 8), (1250, 16), jnp.float32)
        tbl_9 = 0.05 * jax.random.normal(jax.random.fold_in(_tk, 500 + 9), (1250, 16), jnp.float32)
        tbl_10 = 0.05 * jax.random.normal(jax.random.fold_in(_tk, 500 + 10), (125000, 16), jnp.float32)
        tbl_11 = 0.05 * jax.random.normal(jax.random.fold_in(_tk, 500 + 11), (125000, 16), jnp.float32)
        tbl_12 = 0.05 * jax.random.normal(jax.random.fold_in(_tk, 500 + 12), (1000, 16), jnp.float32)
        tbl_13 = 0.05 * jax.random.normal(jax.random.fold_in(_tk, 500 + 13), (12500, 16), jnp.float32)
        tbl_14 = 0.05 * jax.random.normal(jax.random.fold_in(_tk, 500 + 14), (1250, 16), jnp.float32)
        tbl_15 = 0.05 * jax.random.normal(jax.random.fold_in(_tk, 500 + 15), (12500, 16), jnp.float32)
        tbl_16 = 0.05 * jax.random.normal(jax.random.fold_in(_tk, 500 + 16), (1000, 16), jnp.float32)
        tbl_17 = 0.05 * jax.random.normal(jax.random.fold_in(_tk, 500 + 17), (1000, 16), jnp.float32)
        tbl_18 = 0.05 * jax.random.normal(jax.random.fold_in(_tk, 500 + 18), (125000, 16), jnp.float32)
        tbl_19 = 0.05 * jax.random.normal(jax.random.fold_in(_tk, 500 + 19), (1000, 16), jnp.float32)
        tbl_20 = 0.05 * jax.random.normal(jax.random.fold_in(_tk, 500 + 20), (125000, 16), jnp.float32)
        tbl_21 = 0.05 * jax.random.normal(jax.random.fold_in(_tk, 500 + 21), (1250, 16), jnp.float32)
        tbl_22 = 0.05 * jax.random.normal(jax.random.fold_in(_tk, 500 + 22), (12500, 16), jnp.float32)
        tbl_23 = 0.05 * jax.random.normal(jax.random.fold_in(_tk, 500 + 23), (1250, 16), jnp.float32)
        tbl_24 = 0.05 * jax.random.normal(jax.random.fold_in(_tk, 500 + 24), (125000, 16), jnp.float32)
        tbl_25 = 0.05 * jax.random.normal(jax.random.fold_in(_tk, 500 + 25), (1000, 16), jnp.float32)
        tbl_26 = 0.05 * jax.random.normal(jax.random.fold_in(_tk, 500 + 26), (12500, 16), jnp.float32)
        tbl_27 = 0.05 * jax.random.normal(jax.random.fold_in(_tk, 500 + 27), (12500, 16), jnp.float32)
        tbl_28 = 0.05 * jax.random.normal(jax.random.fold_in(_tk, 500 + 28), (1000, 16), jnp.float32)
        tbl_29 = 0.05 * jax.random.normal(jax.random.fold_in(_tk, 500 + 29), (12500, 16), jnp.float32)
        tbl_30 = 0.05 * jax.random.normal(jax.random.fold_in(_tk, 500 + 30), (12500, 16), jnp.float32)
        tbl_31 = 0.05 * jax.random.normal(jax.random.fold_in(_tk, 500 + 31), (1000, 16), jnp.float32)
        tbl_32 = 0.05 * jax.random.normal(jax.random.fold_in(_tk, 500 + 32), (125000, 16), jnp.float32)
        tbl_33 = 0.05 * jax.random.normal(jax.random.fold_in(_tk, 500 + 33), (125000, 16), jnp.float32)
        tbl_34 = 0.05 * jax.random.normal(jax.random.fold_in(_tk, 500 + 34), (1000, 16), jnp.float32)
        tbl_35 = 0.05 * jax.random.normal(jax.random.fold_in(_tk, 500 + 35), (12500, 16), jnp.float32)
        tbl_36 = 0.05 * jax.random.normal(jax.random.fold_in(_tk, 500 + 36), (12500, 16), jnp.float32)
        tbl_37 = 0.05 * jax.random.normal(jax.random.fold_in(_tk, 500 + 37), (12500, 16), jnp.float32)
        tbl_38 = 0.05 * jax.random.normal(jax.random.fold_in(_tk, 500 + 38), (1000, 16), jnp.float32)
        _rk = jax.random.fold_in(_tk, 7)
        W_top1 = 0.0606339 * jax.random.normal(jax.random.fold_in(_tk, 801), (272, 512), jnp.float32)
        W_top2 = 0.0441942 * jax.random.normal(jax.random.fold_in(_tk, 802), (512, 256), jnp.float32)
        W_top3 = 0.0625 * jax.random.normal(jax.random.fold_in(_tk, 803), (256, 1), jnp.float32)
        b_top1 = jnp.zeros((512,), jnp.float32)
        b_top2 = jnp.zeros((256,), jnp.float32)
        return (dense_ctx, ids, tbl_0, tbl_1, tbl_2, tbl_3, tbl_4, tbl_5, tbl_6, tbl_7, tbl_8, tbl_9, tbl_10, tbl_11, tbl_12, tbl_13, tbl_14, tbl_15, tbl_16, tbl_17, tbl_18, tbl_19, tbl_20, tbl_21, tbl_22, tbl_23, tbl_24, tbl_25, tbl_26, tbl_27, tbl_28, tbl_29, tbl_30, tbl_31, tbl_32, tbl_33, tbl_34, tbl_35, tbl_36, tbl_37, tbl_38, W_top1, b_top1, W_top2, b_top2, W_top3)
    dense_ctx, ids, tbl_0, tbl_1, tbl_2, tbl_3, tbl_4, tbl_5, tbl_6, tbl_7, tbl_8, tbl_9, tbl_10, tbl_11, tbl_12, tbl_13, tbl_14, tbl_15, tbl_16, tbl_17, tbl_18, tbl_19, tbl_20, tbl_21, tbl_22, tbl_23, tbl_24, tbl_25, tbl_26, tbl_27, tbl_28, tbl_29, tbl_30, tbl_31, tbl_32, tbl_33, tbl_34, tbl_35, tbl_36, tbl_37, tbl_38, W_top1, b_top1, W_top2, b_top2, W_top3 = _rec_inputs()

    def _L0_rec_setup():
        import jax, jax.numpy as jnp
        import numpy as np
        B, F0, D = (256, 39, 16)
        LAYER_SIZES = [128, 128, 128]
        key = jax.random.key(seed)
        ks = jax.random.split(key, 1 + 2 * len(LAYER_SIZES))
        inputs = jax.random.normal(ks[0], (B, F0, D), dtype=jnp.float32)
        out = {'inputs': inputs}
        field_nums = [F0]
        for i, size in enumerate(LAYER_SIZES):
            fk = field_nums[-1]
            fan_in = F0 * fk
            scale = np.sqrt(2.0 / (fan_in + size)).astype(np.float32)
            out[f'w{i}'] = jax.random.normal(ks[1 + 2 * i], (F0, fk, size), dtype=jnp.float32) * scale
            out[f'b{i}'] = jnp.zeros((size,), dtype=jnp.float32)
            field_nums.append(size // 2)
        return out
    _L0_rec_all = _L0_rec_setup()
    _L0_rec_in = {k: v for k, v in _L0_rec_all.items() if k in ('w0', 'w1', 'w2', 'b0', 'b1', 'b2')}
    del _L0_rec_all
    return {'dense_ctx': dense_ctx, 'ids': ids, 'tbl_0': tbl_0, 'tbl_1': tbl_1, 'tbl_2': tbl_2, 'tbl_3': tbl_3, 'tbl_4': tbl_4, 'tbl_5': tbl_5, 'tbl_6': tbl_6, 'tbl_7': tbl_7, 'tbl_8': tbl_8, 'tbl_9': tbl_9, 'tbl_10': tbl_10, 'tbl_11': tbl_11, 'tbl_12': tbl_12, 'tbl_13': tbl_13, 'tbl_14': tbl_14, 'tbl_15': tbl_15, 'tbl_16': tbl_16, 'tbl_17': tbl_17, 'tbl_18': tbl_18, 'tbl_19': tbl_19, 'tbl_20': tbl_20, 'tbl_21': tbl_21, 'tbl_22': tbl_22, 'tbl_23': tbl_23, 'tbl_24': tbl_24, 'tbl_25': tbl_25, 'tbl_26': tbl_26, 'tbl_27': tbl_27, 'tbl_28': tbl_28, 'tbl_29': tbl_29, 'tbl_30': tbl_30, 'tbl_31': tbl_31, 'tbl_32': tbl_32, 'tbl_33': tbl_33, 'tbl_34': tbl_34, 'tbl_35': tbl_35, 'tbl_36': tbl_36, 'tbl_37': tbl_37, 'tbl_38': tbl_38, 'W_top1': W_top1, 'b_top1': b_top1, 'W_top2': W_top2, 'b_top2': b_top2, 'W_top3': W_top3, 'L0_rec_w0': _L0_rec_in['w0'], 'L0_rec_w1': _L0_rec_in['w1'], 'L0_rec_w2': _L0_rec_in['w2'], 'L0_rec_b0': _L0_rec_in['b0'], 'L0_rec_b1': _L0_rec_in['b1'], 'L0_rec_b2': _L0_rec_in['b2']}

def reference(dense_ctx, ids, tbl_0, tbl_1, tbl_2, tbl_3, tbl_4, tbl_5, tbl_6, tbl_7, tbl_8, tbl_9, tbl_10, tbl_11, tbl_12, tbl_13, tbl_14, tbl_15, tbl_16, tbl_17, tbl_18, tbl_19, tbl_20, tbl_21, tbl_22, tbl_23, tbl_24, tbl_25, tbl_26, tbl_27, tbl_28, tbl_29, tbl_30, tbl_31, tbl_32, tbl_33, tbl_34, tbl_35, tbl_36, tbl_37, tbl_38, W_top1, b_top1, W_top2, b_top2, W_top3, L0_rec_w0, L0_rec_w1, L0_rec_w2, L0_rec_b0, L0_rec_b1, L0_rec_b2):
    import jax
    import jax.numpy as jnp

    def _L0_rec_ref(inputs, w0, w1, w2, b0, b1, b2):
        import jax, jax.numpy as jnp
        import numpy as np
        B, F0, D = (256, 39, 16)
        LAYER_SIZES = [128, 128, 128]
        x0 = inputs
        xk = inputs
        params = [(w0, b0), (w1, b1), (w2, b2)]
        n_layers = len(params)
        direct = []
        for idx, (W, b) in enumerate(params):
            z = jnp.einsum('bhd,bkd,hks->bsd', x0, xk, W) + b[None, :, None]
            z = jax.nn.relu(z)
            if idx != n_layers - 1:
                half = z.shape[1] // 2
                xk = z[:, :half, :]
                direct.append(z[:, half:, :])
            else:
                direct.append(z)
        logit = jnp.sum(jnp.concatenate(direct, axis=1), axis=-1)
        return logit
    e = jnp.stack([tbl_0[ids[:, 0]], tbl_1[ids[:, 1]], tbl_2[ids[:, 2]], tbl_3[ids[:, 3]], tbl_4[ids[:, 4]], tbl_5[ids[:, 5]], tbl_6[ids[:, 6]], tbl_7[ids[:, 7]], tbl_8[ids[:, 8]], tbl_9[ids[:, 9]], tbl_10[ids[:, 10]], tbl_11[ids[:, 11]], tbl_12[ids[:, 12]], tbl_13[ids[:, 13]], tbl_14[ids[:, 14]], tbl_15[ids[:, 15]], tbl_16[ids[:, 16]], tbl_17[ids[:, 17]], tbl_18[ids[:, 18]], tbl_19[ids[:, 19]], tbl_20[ids[:, 20]], tbl_21[ids[:, 21]], tbl_22[ids[:, 22]], tbl_23[ids[:, 23]], tbl_24[ids[:, 24]], tbl_25[ids[:, 25]], tbl_26[ids[:, 26]], tbl_27[ids[:, 27]], tbl_28[ids[:, 28]], tbl_29[ids[:, 29]], tbl_30[ids[:, 30]], tbl_31[ids[:, 31]], tbl_32[ids[:, 32]], tbl_33[ids[:, 33]], tbl_34[ids[:, 34]], tbl_35[ids[:, 35]], tbl_36[ids[:, 36]], tbl_37[ids[:, 37]], tbl_38[ids[:, 38]]], axis=1)
    z = _L0_rec_ref(e, L0_rec_w0, L0_rec_w1, L0_rec_w2, L0_rec_b0, L0_rec_b1, L0_rec_b2)
    z = z.reshape(z.shape[0], -1)
    h = jnp.concatenate([z, dense_ctx], axis=1)
    h = jnp.maximum(h @ W_top1 + b_top1, 0.0)
    h = jnp.maximum(h @ W_top2 + b_top2, 0.0)
    y = h @ W_top3
    return y

_drawn_inputs = setup_inputs


def setup_inputs(seed=0):
    import zlib

    import numpy as np

    out = dict(_drawn_inputs(seed))
    spreads = {'b_top1': (0.0, 2.0),
     'b_top2': (0.0, 2.0),
     'L0_rec_b0': (0.0, 0.344),
     'L0_rec_b1': (0.0, 0.524),
     'L0_rec_b2': (0.0, 0.8)}
    factors = {'tbl_0': 8.0,
     'tbl_1': 8.0,
     'tbl_2': 8.0,
     'tbl_3': 8.0,
     'tbl_4': 8.0,
     'tbl_5': 8.0,
     'tbl_6': 8.0,
     'tbl_7': 8.0,
     'tbl_8': 8.0,
     'tbl_9': 8.0,
     'tbl_10': 8.0,
     'tbl_11': 8.0,
     'tbl_12': 8.0,
     'tbl_13': 8.0,
     'tbl_14': 8.0,
     'tbl_15': 8.0,
     'tbl_16': 8.0,
     'tbl_17': 8.0,
     'tbl_18': 8.0,
     'tbl_19': 8.0,
     'tbl_20': 8.0,
     'tbl_21': 8.0,
     'tbl_22': 8.0,
     'tbl_23': 8.0,
     'tbl_24': 8.0,
     'tbl_25': 8.0,
     'tbl_26': 8.0,
     'tbl_27': 8.0,
     'tbl_28': 8.0,
     'tbl_29': 8.0,
     'tbl_30': 8.0,
     'tbl_31': 8.0,
     'tbl_32': 8.0,
     'tbl_33': 8.0,
     'tbl_34': 8.0,
     'tbl_35': 8.0,
     'tbl_36': 8.0,
     'tbl_37': 8.0,
     'tbl_38': 8.0,
     'L0_rec_w0': 8.0,
     'L0_rec_w1': 6.13,
     'L0_rec_w2': 4.715,
     'dense_ctx': 8.0}
    for name, (base, spread) in spreads.items():
        noise = np.random.default_rng([zlib.crc32(name.encode()), seed]).standard_normal(out[name].shape)
        drawn = base * np.exp(spread * noise) if base else spread * noise
        out[name] = jnp.asarray(drawn.astype(out[name].dtype))
    for name, factor in factors.items():
        out[name] = (out[name] * factor).astype(out[name].dtype)
    return out
```

```python
import numpy as np
import concourse.bass as bass
from concourse import mybir
from concourse.alu_op_type import AluOpType as ALU
from contextlib import ExitStack

BATCH, FIELDS, DIM = 2048, 39, 16
MAPS = 128
HALF = MAPS // 2
ROWS = 128
GROUPS = BATCH // ROWS
CHAN = DIM // 2
COLS = ROWS * CHAN
BANK = 512
CHUNKS = 2 * GROUPS
SHIFTS = FIELDS // 2 + 1
PER0 = 3
N0 = -(-SHIFTS // PER0)
N1 = -(-FIELDS // 2)
TILES = N1 + N0 + N1
LO = 64
SPLIT = LO + FIELDS
TRIPLE = FIELDS * PER0
PERIODIC = N1 * MAPS
BACK = PERIODIC + TRIPLE + PER0 * (N0 - 1)
PICK_W = BACK + TRIPLE
D1, D2, D3, DENSE = 272, 512, 256, 16
PAIRED = range(0, N1)
SQUARED = range(N1, N1 + N0)
LAST = range(N1 + N0, TILES)

PLAN = "FFFFFFFFFFFFFFFFFFFFFFFFFFFFFFFFFFFFFFFFFFFFFFF"
LAG = 3
SUB = 2
NF, NR, NS = 6, 0, 0
OFFSET = 9


def layer_of(j):
    return 1 if j in PAIRED else 0 if j in SQUARED else 2


def rows_of(j):
    if j in SQUARED:
        u = j - N1
        return FIELDS * min(PER0, SHIFTS - PER0 * u)
    t = j if j in PAIRED else j - N1 - N0
    return HALF * min(2, FIELDS - 2 * t)


def rank(j, kinds):
    return sum(PLAN[i] in kinds for i in range(j))


def earlier(j, kinds, ring):
    mine = rank(j, kinds) % ring
    for i in reversed(range(j)):
        if PLAN[i] in kinds and rank(i, kinds) % ring == mine:
            return 0, i
    for i in reversed(range(TILES)):
        if PLAN[i] in kinds and rank(i, kinds) % ring == mine:
            return 1, i


class Turn:

    def __init__(self, loop, plus):
        self.loop, self.plus = loop, plus
        self.fixed, self.odd = loop is None, plus % 2

    def shift(self, n):
        return Turn(self.loop, self.plus + n)

    def number(self):
        return self.plus

    def real(self):
        return not self.fixed or 0 <= self.plus < CHUNKS

    def count(self, per, plus):
        return self.linear(2 * per, per * self.plus + plus)

    def group(self, per, plus):
        return self.linear(per, per * (self.plus // 2) + plus)

    def linear(self, per, plus):
        return plus if self.fixed else self.loop * per + plus


def turns(engine, emit, loops=GROUPS - 1):
    for j in range(TILES):
        emit(Turn(None, -1), j)
    for p in range(2 * TILES + OFFSET):
        emit(Turn(None, p // TILES), p % TILES)
    with engine.Fori(1, loops) as g:
        for p in range(OFFSET, OFFSET + 2 * TILES):
            emit(Turn(g, p // TILES), p % TILES)
    for p in range(2 * loops * TILES + OFFSET, CHUNKS * TILES + OFFSET):
        emit(Turn(None, p // TILES), p % TILES)


def build(nc, a, out):
    f32, f32r, i32 = mybir.dt.float32, mybir.dt.float32r, mybir.dt.int32
    ACT, AX = mybir.ActivationFunctionType, mybir.AxisListType
    SPLITS = "VG"
    plan_f, plan_r = PLAN.count("F"), TILES - PLAN.count("F")
    first_r = sum(PLAN[j] in SPLITS for j in SQUARED)

    ctx = ExitStack()
    with ctx:
        def sb(name, shape, dt=f32):
            return ctx.enter_context(nc.sbuf_tensor(name, shape, dt))

        def ps(name, banks):
            return ctx.enter_context(nc.psum_tensor(name, [128, banks * BANK], f32))

        def sem(name):
            return ctx.enter_context(nc.semaphore(name))

        spread = sb("spread", [128, N1, COLS])
        w_plain = sb("w_plain", [128, max(plan_f, 1), MAPS])
        w_high = sb("w_high", [128, max(plan_r, 1), MAPS], f32r)
        w_low = sb("w_low", [128, max(plan_r, 1), MAPS], f32r)
        pick = sb("pick", [SPLIT, PICK_W], f32r)
        ident = sb("ident", [128, 128])
        bias = sb("bias", [128, 3])
        mark = sb("mark", [128, 2])
        rows_id = sb("rows_id", [ROWS, FIELDS], i32)
        landed = sb("landed", [ROWS, FIELDS, DIM])
        rows_x = sb("rows_x", [ROWS, FIELDS, DIM])
        x_split = sb("x_split", [SPLIT, COLS], f32r)
        x_thrice = sb("x_thrice", [TRIPLE, COLS])
        maps1 = sb("maps1", [128, COLS])
        direct01 = sb("direct01", [128, COLS])
        direct2 = sb("direct2", [128, COLS])
        sums = sb("sums", [128, 2, 2, ROWS])
        feats = sb("feats", [128, 2, BATCH])
        prod_f = sb("prod_f", [128, NF, COLS])
        if plan_r:
            prod_r = sb("prod_r", [128, NR, COLS])
            high = sb("high", [128, NS, COLS], f32r)
            low = sb("low", [128, NS, COLS], f32r)

        zacc = [ps("zacc_a", 2), ps("zacc_b", 2)]
        maps2 = ps("maps2", 2)
        side = [ps("side_a", 1), ps("side_b", 1)]

        s_const = sem("s_const")
        s_wload = sem("s_wload")
        s_zero = sem("s_zero")
        s_prep = sem("s_prep")
        s_fold = sem("s_fold")
        s_ids = sem("s_ids")
        s_mark = sem("s_mark")
        s_gather = sem("s_gather")
        s_rows = sem("s_rows")
        s_side = sem("s_side")
        s_high = sem("s_high")
        s_low = sem("s_low")
        s_thrice = sem("s_thrice")
        s_spread = sem("s_spread")
        s_prod = sem("s_prod")
        s_square = sem("s_square")
        s_round = sem("s_round")
        s_lowv = sem("s_lowv")
        s_lowg = sem("s_lowg")
        s_mm = sem("s_mm")
        s_z0 = sem("s_z0")
        s_z1 = sem("s_z1")
        s_z2 = sem("s_z2")
        s_sum01 = sem("s_sum01")
        s_sum2 = sem("s_sum2")
        s_feat = sem("s_feat")
        s_mlp = sem("s_mlp")
        s_dense = sem("s_dense")
        s_dense_c = sem("s_dense_c")
        s_h = sem("s_h")
        s_hc = sem("s_hc")
        s_out = sem("s_out")

        def n_kind(turn, j, kinds):
            at_start = sum(PLAN[i] in kinds for i in SQUARED)
            if turn.fixed and turn.number() < 0:
                return rank(j, kinds) - rank(N1, kinds)
            if turn.fixed and turn.number() == CHUNKS - 1 and j in LAST:
                return turn.count(rank(TILES, kinds), rank(j, kinds))
            return turn.count(rank(TILES, kinds), at_start + rank(j, kinds))

        def n_tile(turn, j):
            return n_kind(turn, j, "FVG")

        def n_prod(turn, j):
            return turn.count(2 * N1, j if j in PAIRED else j - N0)

        def n_square(turn, j):
            return turn.shift(1).count(2 * N0, 2 * (j - N1))

        def n_side(turn, use):
            return turn.count(SIDES, use)

        TURN_X, THRICE, SQUARE_X, SPREAD_X = 0, 2, 4, 4 + 2 * N0
        SIDES = SPREAD_X + 2 * N1

        def has(turn, j):
            if j in SQUARED:
                return turn.shift(1).real()
            return turn.real()

        def before(turn, j, kinds, ring):
            back, i = earlier(j, kinds, ring)
            then = turn.shift(-back) if back else turn
            if then.fixed and not has(then, i):
                return before(then, i, kinds, ring) if then.number() >= 0 or i in LAST else None
            return then, i

        def slot(j, kinds, ring):
            return rank(j, kinds) % ring

        staged = spread[:, :, :].rearrange("p t c -> p (t c)")
        st0a = staged[:, 0:N0 * MAPS].rearrange("p (t s) -> p t s", s=MAPS)
        st0b = staged[:, N0 * MAPS:2 * N0 * MAPS].rearrange("p (t s) -> p t s", s=MAPS)
        st1 = staged[:, 2 * N0 * MAPS:(2 * N0 + N1) * MAPS].rearrange("p (t s) -> p t s", s=MAPS)
        st2 = staged[:, (2 * N0 + N1) * MAPS:(2 * N0 + 2 * N1) * MAPS].rearrange("p (t s) -> p t s", s=MAPS)
        st_pick = staged[0:SPLIT, 8192:8192 + PICK_W]
        at = [0]

        def mlp(parts, n):
            at[0] += n
            return staged[0:parts, at[0] - n:at[0]]
        m_w1 = mlp(128, 2 * D2).rearrange("p (t n) -> p t n", t=2)
        m_w1d = mlp(DENSE, D2)
        m_w2 = mlp(128, 4 * D3).rearrange("p (t n) -> p t n", t=4)
        m_w3 = mlp(128, 2)
        m_b1 = mlp(128, 4)
        m_b2 = mlp(128, 2)
        m_dense = mlp(128, GROUPS * DENSE).rearrange("p (g e) -> p g e", e=DENSE)
        m_ctx = mlp(DENSE, BATCH)
        m_h1 = mlp(128, 2 * 4 * BANK).rearrange("p (b t n) -> p b t n", b=2, t=4)
        m_h2 = mlp(128, 2 * 2 * BANK).rearrange("p (b t n) -> p b t n", b=2, t=2)
        m_y = mlp(1, BATCH)

        def mlp_bank(n, m):
            k = 7 * n + m
            return zacc[k % 4 // 2][:, k % 2 * BANK:(k % 2 + 1) * BANK]

        w0, w1, w2 = a["L0_rec_w0"], a["L0_rec_w1"], a["L0_rec_w2"]
        FULL = N1 - 1
        block = ctx.enter_context(nc.Block())

        @block.sync
        def _(sp):
            n_w = 0
            sp.dma_start(st_pick, a["pick"]).then_inc(s_const, 16)
            sp.dma_start(ident[:, :], a["ident"]).then_inc(s_const, 16)
            for n, b in enumerate(("L0_rec_b0", "L0_rec_b1", "L0_rec_b2")):
                sp.dma_start(bias[:, n:n + 1], a[b].rearrange("(p o) -> p o", o=1)).then_inc(s_const, 16)
            for w, st in ((w1, st1), (w2, st2)):
                flat = w.rearrange("h k s -> (h k) s")
                sp.dma_start(st[:, 0:FULL, :], flat[0:FULL * 128, :].rearrange("(t p) s -> p t s", p=128)
                             ).then_inc(s_wload, 16)
                sp.dma_start(st[0:HALF, FULL, :], flat[FULL * 128:, :]).then_inc(s_wload, 16)
            flat = w0.rearrange("h k s -> (h k) s")
            sp.wait_ge(s_zero, 1)
            for u, s, lo, hi in W0_RUNS:
                f, g = (lo - s) % FIELDS, (lo + PER0 * u) % FIELDS
                for st, start in ((st0a, f * FIELDS + g), (st0b, g * FIELDS + f)):
                    if st is st0b and u == s == 0:
                        continue
                    stop = start + (hi - lo - 1) * (FIELDS + 1) + 1
                    sp.dma_start(st[s * FIELDS + lo:s * FIELDS + hi, u, :], flat[start:stop:FIELDS + 1, :]
                                 ).then_inc(s_wload, 16)
            ids = a["ids"]
            sp.dma_start(rows_id[:, :], ids[0:ROWS, :]).then_inc(s_ids, 16)
            with sp.Fori(1, GROUPS) as g:
                sp.wait_ge(s_gather, g * (16 * FIELDS))
                sp.dma_start(rows_id[:, :], ids[bass.ds(g * ROWS, ROWS), :]).then_inc(s_ids, 16)
            sp.wait_ge(s_prod, 2 * N1 * CHUNKS)
            wt1, wt2 = a["W_top1"], a["W_top2"]
            loads = [
                (m_w1[0:HALF, 0, :], wt1[HALF:2 * HALF, :]), (m_w1[HALF:128, 0, :], wt1[0:HALF, :]),
                (m_w1[:, 1, :], wt1[MAPS:2 * MAPS, :]), (m_w1d, wt1[2 * MAPS:D1, :]),
                (m_w2, wt2.rearrange("(t p) n -> p t n", p=128)),
                (m_w3, a["W_top3"].rearrange("(t p) o -> p (t o)", p=128)),
                (m_b1, a["b_top1"].rearrange("(t p) -> p t", p=128)),
                (m_b2, a["b_top2"].rearrange("(t p) -> p t", p=128)),
                (m_dense, a["dense_ctx"].rearrange("(g p) e -> p g e", p=128)),
            ]
            assert len(loads) == MLP_LOADS
            for dst, src in loads:
                sp.dma_start(dst, src, allow_slow_non_contiguous=True).then_inc(s_mlp, 16)
            sp.wait_ge(s_hc, 28)
            sp.dma_start(out.rearrange("b o -> o b"), m_y[0:1, :]).then_inc(s_out, 16)
            sp.wait_ge(s_out, 16)

        @block.gpsimd
        def _(pool):
            tables = [a[f"tbl_{f}"] for f in range(FIELDS)]

            nc.gpsimd.memset(mark[:, :], 0.0).then_inc(s_mark, 1)

            def gather(f):
                nc.gpsimd.indirect_dma_start(
                    out=landed[:, f, :], out_offset=None, in_=tables[f],
                    in_offset=bass.IndirectOffsetOnAxis(ap=rows_id[:, f:f + 1], axis=0),
                ).then_inc(s_gather, 16)

            def emit(turn, j):
                if turn.fixed and turn.number() == -1 and j == 0:
                    pool.wait_ge(s_ids, 16)
                    for f in range(FIELDS):
                        gather(f)
                nxt = turn.shift(3 if turn.odd else 2)
                half = FIELDS // 2 + 1
                f = j if turn.odd else half + j
                if nxt.real() and f < (half if turn.odd else FIELDS):
                    if turn.odd and j == 0:
                        pool.wait_ge(s_ids, nxt.group(16, 16))
                        pool.wait_ge(s_rows, nxt.group(1, 0))
                        pool.wait_ge(s_mark, nxt.group(1, 0))
                        nc.gpsimd.tensor_tensor(mark[:, 0:1], mark[:, 0:1], mark[:, 1:2], ALU.add
                                                ).then_inc(s_mark, 1)
                    gather(f)
                if PLAN[j] == "G" and has(turn, j):
                    s = slot(j, SPLITS, NS)
                    p = slot(j, SPLITS, NR)
                    rows = rows_of(j)
                    pool.wait_ge(s_round, n_kind(turn, j, SPLITS) + 1)
                    was = before(turn, j, SPLITS, NS)
                    if was:
                        pool.wait_ge(s_mm, n_tile(*was) + 1)
                    nc.gpsimd.tensor_tensor(low[0:rows, s, :], prod_r[0:rows, p, :], high[0:rows, s, :],
                                            ALU.subtract).then_inc(s_lowg, 1)

            turns(pool, emit, GROUPS - 2)

        @block.scalar
        def _(act):
            def take(turn, layer):
                z = zacc[(turn.odd + {1: 0, 0: 1, 2: 0}[layer]) % 2]
                b = bias[:, layer:layer + 1]
                if layer == 2:
                    act.wait_ge(s_mm, n_tile(turn, TILES - 1) + 1)
                    if not turn.fixed or turn.number() > 0:
                        act.wait_ge(s_sum2, turn.count(1, 0))
                    nc.scalar.activation(direct2[:, :], z[:, :], ACT.Relu, bias=b).then_inc(s_z2, 1)
                    return
                if layer == 0:
                    act.wait_ge(s_mm, n_tile(turn, N1 + N0 - 1) + 1)
                    if turn.real():
                        act.wait_ge(s_prod, turn.count(2 * N1, N1))
                        act.wait_ge(s_sum01, turn.count(1, 1))
                    to, keep, s = maps1, HALF, s_z0
                else:
                    act.wait_ge(s_mm, n_tile(turn, N1 - 1) + 1)
                    if not turn.fixed or turn.number() > 0:
                        act.wait_ge(s_prod, turn.count(2 * N1, 0))
                        act.wait_ge(s_sum01, turn.count(1, 0))
                    to, keep, s = maps2, 0, s_z1
                nc.scalar.activation(to[0:HALF, :], z[0:HALF, :], ACT.Relu, bias=b[0:HALF, :])
                nc.scalar.activation(to[HALF:128, :], z[0:HALF, :], ACT.Relu, bias=b[0:HALF, :])
                nc.scalar.activation(direct01[keep:keep + HALF, :], z[HALF:128, :], ACT.Relu,
                                     bias=b[HALF:128, :]).then_inc(s, 1)

            def spread_tile(turn, t):
                nxt = turn.shift(1)
                rows = rows_of(t)
                for hf in range(2):
                    use = SPREAD_X + 2 * t + hf
                    act.wait_ge(s_side, n_side(nxt, use) + 1)
                    if turn.real() and hf == 0:
                        act.wait_ge(s_prod, n_prod(turn, N1 + N0 + t) + 1)
                    nc.scalar.activation(spread[0:rows, t, hf * BANK:(hf + 1) * BANK],
                                         side[use % 2][0:rows, :], ACT.Copy).then_inc(s_spread, 1)

            def emit(turn, j):
                nxt, last = turn.shift(1), turn.shift(-1)
                if turn.fixed and turn.number() == -1 and j == 0:
                    act.wait_ge(s_gather, 16 * FIELDS)
                    nc.scalar.activation(rows_x[:, :, :], landed[:, :, :], ACT.Copy).then_inc(s_rows, 1)
                    act.wait_ge(s_const, 16 * 5)
                    act.wait_ge(s_prep, 1)
                    act.wait_ge(s_zero, 2)
                if PLAN[j] in SPLITS and has(turn, j):
                    s, p, rows = slot(j, SPLITS, NS), slot(j, SPLITS, NR), rows_of(j)
                    if j in SQUARED:
                        act.wait_ge(s_square, n_square(turn, j) + 2)
                    else:
                        act.wait_ge(s_prod, n_prod(turn, j) + 1)
                    was = before(turn, j, SPLITS, NS)
                    if was:
                        act.wait_ge(s_mm, n_tile(*was) + 1)
                    nc.scalar.activation(high[0:rows, s, :], prod_r[0:rows, p, :], ACT.Copy
                                         ).then_inc(s_round, 1)
                if nxt.real():
                    if j in (1 + LAG, 3 + LAG):
                        hf = (j - 1 - LAG) // 2
                        act.wait_ge(s_side, n_side(nxt, TURN_X + hf) + 1)
                        nc.scalar.activation(x_split[0:FIELDS, hf * BANK:(hf + 1) * BANK],
                                             side[hf][0:FIELDS, :], ACT.Copy).then_inc(s_high, 1)
                    if j in (8 + LAG, 9 + LAG):
                        hf = j - 8 - LAG
                        act.wait_ge(s_side, n_side(nxt, THRICE + hf) + 1)
                        if turn.real():
                            act.wait_ge(s_square, turn.count(2 * N0, 2 * N0))
                        nc.scalar.activation(x_thrice[:, hf * BANK:(hf + 1) * BANK],
                                             side[hf][0:TRIPLE, :], ACT.Copy).then_inc(s_thrice, 1)
                    if j == N1 + N0 - 1 + LAG:
                        take(turn, 0)
                    t = j - N1 - N0 - LAG
                    if 0 <= t:
                        spread_tile(turn, t)
                if j < LAG and turn.real():
                    spread_tile(last, N1 - LAG + j)
                if j == N1 - 1 + LAG and turn.real():
                    take(turn, 1)
                if j == LAG - 1 and last.real():
                    take(last, 2)
                if j == 40 and not turn.odd and turn.shift(2).real():
                    act.wait_ge(s_gather, turn.group(16 * FIELDS, 2 * 16 * FIELDS))
                    act.wait_ge(s_side, n_side(nxt, TURN_X + 1) + 1)
                    nc.scalar.activation(rows_x[:, :, :], landed[:, :, :], ACT.Copy).then_inc(s_rows, 1)

            turns(act, emit)

            act.wait_ge(s_mlp, 16 * MLP_LOADS)
            for n in range(4):
                act.wait_ge(s_dense, n + 1)
                nc.scalar.activation(m_ctx[:, n * BANK:(n + 1) * BANK], side[n % 2][0:DENSE, :], ACT.Copy
                                     ).then_inc(s_dense_c, 1)
            for n in range(4):
                for m in range(7):
                    act.wait_ge(s_h, 7 * n + m + 1)
                    bank = mlp_bank(n, m)
                    if m < 4:
                        nc.scalar.activation(m_h1[:, n % 2, m, :], bank, ACT.Relu, bias=m_b1[:, m:m + 1]
                                             ).then_inc(s_hc, 1)
                    elif m < 6:
                        nc.scalar.activation(m_h2[:, n % 2, m - 4, :], bank, ACT.Relu, bias=m_b2[:, m - 4:m - 3]
                                             ).then_inc(s_hc, 1)
                    else:
                        nc.scalar.activation(m_y[0:1, n * BANK:(n + 1) * BANK], bank[0:1, :], ACT.Copy
                                             ).then_inc(s_hc, 1)

        @block.vector
        def _(dve):
            nc.vector.memset(st0b[:, 0, :], 0.0).then_inc(s_zero, 1)
            nc.vector.memset(x_split[32:64, :].bitcast(f32), 0.0).then_inc(s_zero, 1)
            dve.wait_ge(s_const, 16 * 5)
            nc.vector.tensor_copy(pick[:, :], st_pick)
            dve.wait_ge(s_wload, 16 * N_WLOADS)
            nc.vector.tensor_tensor(st0a[0:TRIPLE, 0:N0 - 1, :], st0a[0:TRIPLE, 0:N0 - 1, :], st0b[0:TRIPLE, 0:N0 - 1, :],
                                    ALU.add)
            tail = rows_of(N1 + N0 - 1)
            nc.vector.tensor_tensor(st0a[0:tail, N0 - 1, :], st0a[0:tail, N0 - 1, :], st0b[0:tail, N0 - 1, :],
                                    ALU.add).then_inc(s_fold, 1)
            dve.wait_ge(s_fold, 1)
            for j in range(TILES):
                rows = rows_of(j)
                src = (st1[0:rows, j, :] if j in PAIRED else st0a[0:rows, j - N1, :] if j in SQUARED
                       else st2[0:rows, j - N1 - N0, :])
                if PLAN[j] == "F":
                    last = nc.vector.tensor_copy(w_plain[0:rows, rank(j, "F"), :], src)
                else:
                    last = nc.vector.tensor_copy(w_high[0:rows, rank(j, SPLITS), :], src)
            last.then_inc(s_fold, 1)
            dve.wait_ge(s_fold, 2)
            for j in range(TILES):
                rows = rows_of(j)
                src = (st1[0:rows, j, :] if j in PAIRED else st0a[0:rows, j - N1, :] if j in SQUARED
                       else st2[0:rows, j - N1 - N0, :])
                if PLAN[j] != "F":
                    r = rank(j, SPLITS)
                    last = nc.vector.tensor_tensor(w_low[0:rows, r, :], src, w_high[0:rows, r, :], ALU.subtract)
            if plan_r:
                last.then_inc(s_fold, 1)
                dve.wait_ge(s_fold, 3)
            nc.vector.memset(sums[:, :, :, :], 0.0).then_inc(s_prep, 1)

            def low_part(turn, j):
                s, p, rows = slot(j, SPLITS, NS), slot(j, SPLITS, NR), rows_of(j)
                dve.wait_ge(s_round, n_kind(turn, j, SPLITS) + 1)
                was = before(turn, j, SPLITS, NS)
                if was:
                    dve.wait_ge(s_mm, n_tile(*was) + 1)
                nc.vector.tensor_tensor(low[0:rows, s, :], prod_r[0:rows, p, :], high[0:rows, s, :],
                                        ALU.subtract).then_inc(s_lowv, 1)

            def product(turn, j):
                rows = rows_of(j)
                if PLAN[j] == "F":
                    to = prod_f[0:rows, slot(j, "F", NF), :]
                    was = before(turn, j, "F", NF)
                    if was:
                        dve.wait_ge(s_mm, n_tile(*was) + 1)
                else:
                    to = prod_r[0:rows, slot(j, SPLITS, NR), :]
                    was = before(turn, j, SPLITS, NR)
                    if was:
                        k = PLAN[was[1]]
                        dve.wait_ge(s_lowv if k == "V" else s_lowg, n_kind(*was, k) + 1)
                if j in SQUARED:
                    u, nxt = j - N1, turn.shift(1)
                    if u == 0:
                        dve.wait_ge(s_thrice, nxt.count(2, 2))
                    for hf in range(2):
                        use = SQUARE_X + 2 * u + hf
                        dve.wait_ge(s_side, n_side(nxt, use) + 1)
                        nc.vector.tensor_tensor(to[:, hf * BANK:(hf + 1) * BANK], side[use % 2][0:rows, :],
                                                x_thrice[0:rows, hf * BANK:(hf + 1) * BANK], ALU.mult
                                                ).then_inc(s_square, 1)
                    return
                t = j if j in PAIRED else j - N1 - N0
                if j in PAIRED:
                    if t == 0:
                        dve.wait_ge(s_z0, turn.count(1, 1))
                    dve.wait_ge(s_spread, turn.count(2 * N1, 2 * t + 2))
                elif t == 0:
                    dve.wait_ge(s_z1, turn.count(1, 1))
                maps = maps1 if j in PAIRED else maps2
                nc.vector.tensor_tensor(to, spread[0:rows, t, :], maps[0:rows, :], ALU.mult).then_inc(s_prod, 1)

            def channel_sum(turn, which):
                src, ready, done = ((direct01, s_z1, s_sum01), (direct2, s_z2, s_sum2))[which]
                dve.wait_ge(ready, turn.count(1, 1))
                if not turn.odd and (not turn.fixed or turn.number() > 0):
                    dve.wait_ge(s_feat, turn.count(1, 0))
                nc.vector.tensor_reduce(sums[:, which, turn.odd, :],
                                        src[:, :].rearrange("p (d b) -> p b d", b=ROWS), AX.X, ALU.add
                                        ).then_inc(done, 1)

            def feature(turn, which):
                dve.wait_ge((s_sum01, s_sum2)[which], turn.count(1, 1))
                nc.vector.tensor_tensor(feats[:, which, bass.ds(turn.group(ROWS, 0), ROWS)],
                                        sums[:, which, 0, :], sums[:, which, 1, :], ALU.add).then_inc(s_feat, 1)

            def emit(turn, j):
                nxt, last = turn.shift(1), turn.shift(-1)
                if has(turn, j):
                    product(turn, j)
                then, i = (turn, j - SUB) if j >= SUB else (last, j - SUB + TILES)
                if PLAN[i] == "V" and has(then, i):
                    low_part(then, i)
                if nxt.real() and j in (7, 8):
                    hf = j - 7
                    dve.wait_ge(s_high, nxt.count(2, hf + 1))
                    nc.vector.tensor_tensor(x_split[LO:SPLIT, hf * BANK:(hf + 1) * BANK], side[hf][0:FIELDS, :],
                                            x_split[0:FIELDS, hf * BANK:(hf + 1) * BANK], ALU.subtract
                                            ).then_inc(s_low, 1)
                if turn.real() and j == N1 + LAG + 2:
                    channel_sum(turn, 0)
                if turn.real() and turn.odd and j == N1 + LAG + 4:
                    feature(turn, 0)
                if last.real() and j == LAG + 2:
                    channel_sum(last, 1)
                if last.real() and last.odd and j == LAG + 4:
                    feature(last, 1)

            turns(dve, emit)

        @block.tensor
        def _(pe):
            def contract(turn, j):
                layer = layer_of(j)
                z = zacc[(turn.odd + {1: 0, 0: 1, 2: 0}[layer]) % 2]
                rows = rows_of(j)
                of = {1: PAIRED, 0: SQUARED, 2: LAST}[layer]
                first, last = j == of[0], j == of[-1]
                if first and layer == 1:
                    pe.wait_ge(s_z0, turn.count(1, 1))
                    if not turn.fixed or turn.number() > 0:
                        pe.wait_ge(s_z1, turn.count(1, 0))
                if first and layer == 0 and turn.real():
                    if not turn.fixed or turn.number() > 0:
                        pe.wait_ge(s_z2, turn.count(1, 0))
                if first and layer == 2:
                    pe.wait_ge(s_z1, turn.count(1, 1))

                def mm(hf, w, x, start, stop):
                    return nc.tensor.matmul(z[:, hf * BANK:(hf + 1) * BANK], w, x[:, hf * BANK:(hf + 1) * BANK],
                                            start=start, stop=stop)
                if PLAN[j] == "F":
                    if j in SQUARED:
                        pe.wait_ge(s_square, n_square(turn, j) + 2)
                    else:
                        pe.wait_ge(s_prod, n_prod(turn, j) + 1)
                    x = prod_f[0:rows, slot(j, "F", NF), :]
                    for hf in range(2):
                        done = mm(hf, w_plain[0:rows, rank(j, "F"), :], x, first, last)
                else:
                    s, r = slot(j, SPLITS, NS), rank(j, SPLITS)
                    wh, wl = w_high[0:rows, r, :], w_low[0:rows, r, :]
                    pe.wait_ge(s_round, n_kind(turn, j, SPLITS) + 1)
                    for hf in range(2):
                        mm(hf, wl, high[0:rows, s, :], first, False)
                    for hf in range(2):
                        mm(hf, wh, high[0:rows, s, :], False, False)
                    k = PLAN[j]
                    pe.wait_ge(s_lowv if k == "V" else s_lowg, n_kind(turn, j, k) + 1)
                    for hf in range(2):
                        done = mm(hf, wh, low[0:rows, s, :], False, last)
                done.then_inc(s_mm, 1)

            def side_work(turn, j):
                nxt = turn.shift(1)
                if not nxt.real():
                    return
                xh = [x_split[:, hf * BANK:(hf + 1) * BANK] for hf in range(2)]
                if j in (1, 3):
                    hf = (j - 1) // 2
                    if hf == 0:
                        pe.wait_ge(s_rows, nxt.group(1, 1))
                    if turn.real():
                        pe.wait_ge(s_spread, turn.count(2 * N1, 2 * N1 - 1 + hf))
                    for d in range(CHAN // 2):
                        done = nc.tensor.matmul(side[hf][0:FIELDS, d * ROWS:(d + 1) * ROWS],
                                                rows_x[:, :, nxt.odd * CHAN + hf * CHAN // 2 + d], ident[:, :],
                                                start=d == 0, stop=d == CHAN // 2 - 1, skip_group_check=True)
                    done.then_inc(s_side, 1)
                if j in (8, 9):
                    hf = j - 8
                    pe.wait_ge(s_low, nxt.count(2, hf + 1))
                    nc.tensor.matmul(side[hf][0:TRIPLE, :],
                                     pick[:, BACK:BACK + TRIPLE], xh[hf],
                                     start=True, stop=True).then_inc(s_side, 1)
                u = j - N1 + 3
                if 0 <= u < N0:
                    sel = pick[:, PERIODIC + PER0 * u:PERIODIC + PER0 * u + TRIPLE]
                    for hf in range(2):
                        if u == 0:
                            pe.wait_ge(s_thrice, nxt.count(2, hf + 1))
                        else:
                            pe.wait_ge(s_square, nxt.count(2 * N0, 2 * u - 1 + hf))
                        nc.tensor.matmul(side[hf][0:TRIPLE, :], sel, xh[hf],
                                         start=True, stop=True).then_inc(s_side, 1)
                t = j - N1 - N0
                if 0 <= t:
                    for hf in range(2):
                        if t == 0:
                            pe.wait_ge(s_square, nxt.count(2 * N0, 2 * N0 - 1 + hf))
                        else:
                            pe.wait_ge(s_spread, nxt.count(2 * N1, 2 * t - 1 + hf))
                        nc.tensor.matmul(side[hf][:, :], pick[:, t * MAPS:(t + 1) * MAPS], xh[hf],
                                         start=True, stop=True).then_inc(s_side, 1)

            def emit(turn, j):
                if turn.fixed and turn.number() == -1 and j == 0:
                    pe.wait_ge(s_const, 16 * 5)
                    pe.wait_ge(s_prep, 1)
                if has(turn, j):
                    contract(turn, j)
                side_work(turn, j)

            turns(pe, emit)

            pe.wait_ge(s_mlp, 16 * MLP_LOADS)
            for n in range(4):
                if n >= 2:
                    pe.wait_ge(s_dense_c, n - 1)
                for g in range(4):
                    done = nc.tensor.matmul(side[n % 2][0:DENSE, g * ROWS:(g + 1) * ROWS], m_dense[:, 4 * n + g, :],
                                            ident[:, :], start=g == 0, stop=g == 3, skip_group_check=True)
                done.then_inc(s_dense, 1)
            pe.wait_ge(s_feat, 2 * GROUPS)
            pe.wait_ge(s_z2, CHUNKS)
            for n in range(4):
                cols = slice(n * BANK, (n + 1) * BANK)
                for m in range(7):
                    k = 7 * n + m
                    if m == 0:
                        pe.wait_ge(s_dense_c, n + 1)
                    if m in (4, 6):
                        pe.wait_ge(s_hc, k)
                    elif k >= 4:
                        pe.wait_ge(s_hc, k - 3)
                    bank = mlp_bank(n, m)
                    if m < 4:
                        ms = slice(m * 128, (m + 1) * 128)
                        nc.tensor.matmul(bank, m_w1[:, 0, ms], feats[:, 0, cols], start=True, stop=False)
                        nc.tensor.matmul(bank, m_w1[:, 1, ms], feats[:, 1, cols], start=False, stop=False)
                        done = nc.tensor.matmul(bank, m_w1d[:, ms], m_ctx[:, cols], start=False, stop=True)
                    elif m < 6:
                        ms = slice((m - 4) * 128, (m - 3) * 128)
                        for q in range(4):
                            done = nc.tensor.matmul(bank, m_w2[:, q, ms], m_h1[:, n % 2, q, :],
                                                    start=q == 0, stop=q == 3)
                    else:
                        for q in range(2):
                            done = nc.tensor.matmul(bank[0:1, :], m_w3[:, q:q + 1], m_h2[:, n % 2, q, :],
                                                    start=q == 0, stop=q == 1)
                    done.then_inc(s_h, 1)


MLP_LOADS = 9


def w0_runs():
    runs = []
    for j in range(SHIFTS):
        u, s = divmod(j, PER0)
        cuts = sorted({0, s, FIELDS - PER0 * u, FIELDS})
        runs += [(u, s, lo, hi) for lo, hi in zip(cuts, cuts[1:])]
    return runs


W0_RUNS = w0_runs()
N_WLOADS = 4 + 2 * len(W0_RUNS) - sum(u == s == 0 for u, s, _, _ in W0_RUNS)


def selections():
    pick = np.zeros((SPLIT, PICK_W), np.float32)
    for at in (0, LO):
        for f in range(FIELDS):
            pick[at + f, f * HALF:(f + 1) * HALF] = 1.0
            pick[at + f, PERIODIC + f:BACK:FIELDS] = 1.0
            for s in range(PER0):
                pick[at + f, BACK + s * FIELDS + (f + s) % FIELDS] = 1.0
    return pick


def kernel(**inputs):
    import concourse.bacc as _bacc
    from concourse.bass_utils import run_bass_kernel_spmd as _run

    nc = _bacc.Bacc("TRN2", target_bir_lowering=False, num_devices=1)
    arrays, args = {}, {}
    given = {name: np.ascontiguousarray(x) for name, x in inputs.items()}
    given["pick"] = selections()
    given["ident"] = np.eye(128, dtype=np.float32)
    for name, x in given.items():
        arrays[f"in_{name}"] = x
        args[name] = nc.dram_tensor(f"in_{name}", x.shape, mybir.dt.from_np(x.dtype), kind="ExternalInput").ap()
    out = nc.dram_tensor("out", (BATCH, 1), mybir.dt.float32, kind="ExternalOutput").ap()
    build(nc, args, out)
    return _run(nc, [arrays], core_ids=[0]).results[0]["out"]
```

```python
import numpy as np
import concourse.bass as bass
from concourse import mybir
from concourse.alu_op_type import AluOpType as ALU
from contextlib import ExitStack

BATCH, FIELDS, DIM = 2048, 39, 16
MAPS = 128
HALF = MAPS // 2
ROWS = 128
GROUPS = BATCH // ROWS
CHAN = DIM // 2
COLS = ROWS * CHAN
BANK = 512
CHUNKS = 2 * GROUPS
SHIFTS = FIELDS // 2 + 1
PER0 = 3
N0 = -(-SHIFTS // PER0)
N1 = -(-FIELDS // 2)
TILES = N1 + N0 + N1
LO = 64
SPLIT = LO + FIELDS
TRIPLE = FIELDS * PER0
PERIODIC = N1 * MAPS
BACK = PERIODIC + TRIPLE + PER0 * (N0 - 1)
PICK_W = BACK + TRIPLE
D1, D2, D3, DENSE = 272, 512, 256, 16
PAIRED = range(0, N1)
SQUARED = range(N1, N1 + N0)
LAST = range(N1 + N0, TILES)

PLAN = "FVFVFFVFVFFVFVFFVFVFFVFFFVFVFVVFVVFVFVVFVVFVVFV"
NP, NH, NL, LATE, LZ, LAG, SUB, AHEAD = 5, 3, 3, 2, 4, 2, 2, 4
OFFSET = 12


def layer_of(j):
    return 1 if j in PAIRED else 0 if j in SQUARED else 2


def rows_of(j):
    if j in SQUARED:
        u = j - N1
        return FIELDS * min(PER0, SHIFTS - PER0 * u)
    t = j if j in PAIRED else j - N1 - N0
    return HALF * min(2, FIELDS - 2 * t)


def rank(j, kinds):
    return sum(PLAN[i] in kinds for i in range(j))


def slot(j, kinds, ring):
    short = -rank(TILES, kinds) % ring
    whole = rank(TILES, kinds) - short * (ring - 1)
    assert whole >= 0
    r = rank(j, kinds)
    return r % ring if r < whole else (r - whole) % (ring - 1)


def earlier(j, kinds, ring):
    for back, upto in ((0, j), (1, TILES)):
        for i in reversed(range(upto)):
            if PLAN[i] in kinds and slot(i, kinds, ring) == slot(j, kinds, ring):
                return back, i


class Turn:

    def __init__(self, loop, plus):
        self.loop, self.plus = loop, plus
        self.fixed, self.odd = loop is None, plus % 2

    def shift(self, n):
        return Turn(self.loop, self.plus + n)

    def number(self):
        return self.plus

    def real(self):
        return not self.fixed or 0 <= self.plus < CHUNKS

    def count(self, per, plus):
        return self.linear(2 * per, per * self.plus + plus)

    def group(self, per, plus):
        return self.linear(per, per * (self.plus // 2) + plus)

    def linear(self, per, plus):
        return plus if self.fixed else self.loop * per + plus


def turns(engine, emit, loops=GROUPS - 1):
    for j in range(TILES):
        emit(Turn(None, -1), j)
    for p in range(2 * TILES + OFFSET):
        emit(Turn(None, p // TILES), p % TILES)
    with engine.Fori(1, loops) as g:
        for p in range(OFFSET, OFFSET + 2 * TILES):
            emit(Turn(g, p // TILES), p % TILES)
    for p in range(2 * loops * TILES + OFFSET, CHUNKS * TILES + OFFSET):
        emit(Turn(None, p // TILES), p % TILES)


def build(nc, a, out):
    f32, f32r, i32 = mybir.dt.float32, mybir.dt.float32r, mybir.dt.int32
    ACT, AX = mybir.ActivationFunctionType, mybir.AxisListType
    ALL, SPLITS = "FVG", "VG"
    plan_f, plan_r = PLAN.count("F"), TILES - PLAN.count("F")
    first_r = sum(PLAN[j] in SPLITS for j in SQUARED)

    kept = nc.dram_tensor("features", (GROUPS, 128, 2 * ROWS), f32, kind="Internal").ap()

    ctx = ExitStack()
    with ctx:
        def sb(name, shape, dt=f32):
            return ctx.enter_context(nc.sbuf_tensor(name, shape, dt))

        def ps(name, banks):
            return ctx.enter_context(nc.psum_tensor(name, [128, banks * BANK], f32))

        def sem(name):
            return ctx.enter_context(nc.semaphore(name))

        spread = sb("spread", [128, N1, COLS])
        w_plain = sb("w_plain", [128, max(plan_f, 1), MAPS])
        w_high = sb("w_high", [128, max(plan_r, 1), MAPS], f32r)
        w_low = sb("w_low", [128, max(plan_r, 1), MAPS], f32r)
        pick = sb("pick", [SPLIT, PICK_W], f32r)
        ident = sb("ident", [128, 128])
        bias = sb("bias", [128, 3])
        mark = sb("mark", [128, 2])
        rows_id = sb("rows_id", [ROWS, FIELDS], i32)
        landed = sb("landed", [ROWS, FIELDS, DIM])
        rows_x = sb("rows_x", [ROWS, FIELDS, DIM])
        x_split = sb("x_split", [SPLIT, COLS], f32r)
        x_thrice = sb("x_thrice", [TRIPLE, COLS])
        maps1 = sb("maps1", [128, COLS])
        maps2 = sb("maps2", [128, COLS])
        direct01 = sb("direct01", [128, COLS])
        direct2 = sb("direct2", [128, COLS])
        sums = sb("sums", [128, 2, 2, ROWS])
        feat = sb("feat", [128, 2, ROWS])
        prod = sb("prod", [128, NP, COLS])
        if plan_r:
            high = sb("high", [128, NH, COLS], f32r)
            low = sb("low", [128, NL, COLS], f32r)

        zacc = [ps("zacc_a", 2), ps("zacc_b", 2)]
        sides = [ps("side_a", 2), ps("side_b", 2)]

        s_const = sem("s_const")
        s_wload = sem("s_wload")
        s_zero = sem("s_zero")
        s_prep = sem("s_prep")
        s_fold = sem("s_fold")
        s_ids = sem("s_ids")
        s_mark = sem("s_mark")
        s_gather = sem("s_gather")
        s_rows = sem("s_rows")
        s_side = sem("s_side")
        s_high = sem("s_high")
        s_low = sem("s_low")
        s_thrice = sem("s_thrice")
        s_spread = sem("s_spread")
        s_prod = sem("s_prod")
        s_square = sem("s_square")
        s_round = sem("s_round")
        s_lowv = sem("s_lowv")
        s_lowg = sem("s_lowg")
        s_mm = sem("s_mm")
        s_z0 = sem("s_z0")
        s_z1 = sem("s_z1")
        s_z2 = sem("s_z2")
        s_sum01 = sem("s_sum01")
        s_sum2 = sem("s_sum2")
        s_feat = sem("s_feat")
        s_kept = sem("s_kept")
        s_feats = [sem(f"s_feats{n}") for n in range(4)]
        s_mlp = sem("s_mlp")
        s_dense = sem("s_dense")
        s_dense_c = sem("s_dense_c")
        s_h = sem("s_h")
        s_hc = sem("s_hc")
        s_out = sem("s_out")

        def n_kind(turn, j, kinds):
            at_start = sum(PLAN[i] in kinds for i in SQUARED)
            if turn.fixed and turn.number() < 0:
                return rank(j, kinds) - rank(N1, kinds)
            if turn.fixed and turn.number() == CHUNKS - 1 and j in LAST:
                return turn.count(rank(TILES, kinds), rank(j, kinds))
            return turn.count(rank(TILES, kinds), at_start + rank(j, kinds))

        def n_tile(turn, j, plus=0):
            if turn.fixed and turn.number() < 0:
                return j - N1 + plus
            missing = N0 - LATE if turn.fixed and turn.number() == CHUNKS - 1 and j in LAST else 0
            return turn.count(TILES, N0 + LATE + j - missing + plus)

        def n_late(turn, j):
            return n_tile(turn, j, LATE)

        def tail(of):
            split = [j for j in of if PLAN[j] in SPLITS]
            return split[-1] if split and split[-1] + LATE >= of[-1] else None

        def n_whole(turn, of):
            end = tail(of)
            extra = 1 + (0 if end is None else end + LATE - of[-1])
            return n_tile(turn, of[-1], extra)

        def step_back(turn, j, n):
            for _ in range(n):
                j -= 1
                if j < 0:
                    turn, j = turn.shift(-1), TILES - 1
                    if turn.fixed and turn.number() < 0:
                        return None
                if not has(turn, j):
                    return None
            return turn, j

        def n_prod(turn, j):
            return turn.count(2 * N1, j if j in PAIRED else j - N0)

        def n_square(turn, j):
            return turn.shift(1).count(N0, j - N1)

        def n_side(turn, use):
            return turn.count(SIDES, use)

        TURN_X, THRICE, SQUARE_X, SPREAD_X = 0, 1, 2, 2 + N0
        SIDES = SPREAD_X + N1

        def side(turn, use):
            return sides[(turn.plus * SIDES + use) % 2]

        def has(turn, j):
            if j in SQUARED:
                return turn.shift(1).real()
            return turn.real()

        def before(turn, j, kinds, ring):
            back, i = earlier(j, kinds, ring)
            then = turn.shift(-back) if back else turn
            if then.fixed and not has(then, i):
                return before(then, i, kinds, ring) if then.number() >= 0 or i in LAST else None
            return then, i

        staged = spread[:, :, :].rearrange("p t c -> p (t c)")
        st0a = staged[:, 0:N0 * MAPS].rearrange("p (t s) -> p t s", s=MAPS)
        st0b = staged[:, N0 * MAPS:2 * N0 * MAPS].rearrange("p (t s) -> p t s", s=MAPS)
        st1 = staged[:, 2 * N0 * MAPS:(2 * N0 + N1) * MAPS].rearrange("p (t s) -> p t s", s=MAPS)
        st2 = staged[:, (2 * N0 + N1) * MAPS:(2 * N0 + 2 * N1) * MAPS].rearrange("p (t s) -> p t s", s=MAPS)
        st_pick = staged[0:SPLIT, 8192:8192 + PICK_W]
        at = [0]

        def mlp(parts, n):
            at[0] += n
            return staged[0:parts, at[0] - n:at[0]]
        m_w1 = mlp(128, 2 * D2).rearrange("p (t n) -> p t n", t=2)
        m_w1d = mlp(DENSE, D2)
        m_w2 = mlp(128, 4 * D3).rearrange("p (t n) -> p t n", t=4)
        m_w3 = mlp(128, 2)
        m_b1 = mlp(128, 4)
        m_b2 = mlp(128, 2)
        m_dense = mlp(128, GROUPS * DENSE).rearrange("p (g e) -> p g e", e=DENSE)
        m_ctx = mlp(DENSE, BATCH)
        m_h1 = mlp(128, 2 * 4 * BANK).rearrange("p (b t n) -> p b t n", b=2, t=4)
        m_h2 = mlp(128, 2 * 2 * BANK).rearrange("p (b t n) -> p b t n", b=2, t=2)
        m_y = mlp(1, BATCH)
        m_feats = mlp(128, GROUPS * 2 * ROWS).rearrange("p (g w b) -> p g w b", g=GROUPS, w=2)

        def mlp_bank(n, m):
            k = 7 * n + m
            return zacc[k % 4 // 2][:, k % 2 * BANK:(k % 2 + 1) * BANK]

        w0, w1, w2 = a["L0_rec_w0"], a["L0_rec_w1"], a["L0_rec_w2"]
        FULL = N1 - 1
        block = ctx.enter_context(nc.Block())

        @block.sync
        def _(sp):
            ids = a["ids"]
            sp.dma_start(rows_id[:, :], ids[0:ROWS, :]).then_inc(s_ids, 16)
            sp.dma_start(st_pick, a["pick"]).then_inc(s_const, 16)
            sp.dma_start(ident[:, :], a["ident"]).then_inc(s_const, 16)
            for n, b in enumerate(("L0_rec_b0", "L0_rec_b1", "L0_rec_b2")):
                sp.dma_start(bias[:, n:n + 1], a[b].rearrange("(p o) -> p o", o=1)).then_inc(s_const, 16)
            for w, st in ((w1, st1), (w2, st2)):
                flat = w.rearrange("h k s -> (h k) s")
                sp.dma_start(st[:, 0:FULL, :], flat[0:FULL * 128, :].rearrange("(t p) s -> p t s", p=128)
                             ).then_inc(s_wload, 16)
                sp.dma_start(st[0:HALF, FULL, :], flat[FULL * 128:, :]).then_inc(s_wload, 16)
            flat = w0.rearrange("h k s -> (h k) s")
            sp.wait_ge(s_zero, 1)
            for u, s, lo, hi in W0_RUNS:
                f, g = (lo - s) % FIELDS, (lo + PER0 * u) % FIELDS
                for st, start in ((st0a, f * FIELDS + g), (st0b, g * FIELDS + f)):
                    if st is st0b and u == s == 0:
                        continue
                    stop = start + (hi - lo - 1) * (FIELDS + 1) + 1
                    sp.dma_start(st[s * FIELDS + lo:s * FIELDS + hi, u, :], flat[start:stop:FIELDS + 1, :]
                                 ).then_inc(s_wload, 16)
            with sp.Fori(1, GROUPS) as g:
                sp.wait_ge(s_gather, g * (16 * FIELDS))
                sp.dma_start(rows_id[:, :], ids[bass.ds(g * ROWS, ROWS), :]).then_inc(s_ids, 16)
            sp.wait_ge(s_prod, 2 * N1 * CHUNKS)
            wt1, wt2 = a["W_top1"], a["W_top2"]
            loads = [
                (m_w1[0:HALF, 0, :], wt1[HALF:2 * HALF, :]), (m_w1[HALF:128, 0, :], wt1[0:HALF, :]),
                (m_w1[:, 1, :], wt1[MAPS:2 * MAPS, :]), (m_w1d, wt1[2 * MAPS:D1, :]),
                (m_w2, wt2.rearrange("(t p) n -> p t n", p=128)),
                (m_w3, a["W_top3"].rearrange("(t p) o -> p (t o)", p=128)),
                (m_b1, a["b_top1"].rearrange("(t p) -> p t", p=128)),
                (m_b2, a["b_top2"].rearrange("(t p) -> p t", p=128)),
                (m_dense, a["dense_ctx"].rearrange("(g p) e -> p g e", p=128)),
            ]
            assert len(loads) == MLP_LOADS
            PER = BANK // ROWS
            for dst, src in loads:
                sp.dma_start(dst, src, allow_slow_non_contiguous=True).then_inc(s_mlp, 16)
            for n in range(4):
                sp.wait_ge(s_kept, 16 * PER * (n + 1))
                sp.dma_start(m_feats[:, PER * n:PER * (n + 1), :, :].rearrange("p g w b -> p g (w b)"),
                             kept[PER * n:PER * (n + 1), :, :].rearrange("g p c -> p g c")).then_inc(s_feats[n], 16)
            sp.wait_ge(s_hc, 28)
            sp.dma_start(out.rearrange("b o -> o b"), m_y[0:1, :]).then_inc(s_out, 16)
            sp.wait_ge(s_out, 16)

        @block.gpsimd
        def _(pool):
            tables = [a[f"tbl_{f}"] for f in range(FIELDS)]

            nc.gpsimd.memset(mark[:, :], 0.0).then_inc(s_mark, 1)

            def gather(f):
                nc.gpsimd.indirect_dma_start(
                    out=landed[:, f, :], out_offset=None, in_=tables[f],
                    in_offset=bass.IndirectOffsetOnAxis(ap=rows_id[:, f:f + 1], axis=0),
                ).then_inc(s_gather, 16)

            def emit(turn, j):
                if turn.fixed and turn.number() == -1 and j == 0:
                    pool.wait_ge(s_ids, 16)
                    for f in range(FIELDS):
                        gather(f)
                nxt = turn.shift(3 if turn.odd else 2)
                half = FIELDS // 2 + 1
                f = j if turn.odd else half + j
                if nxt.real() and f < (half if turn.odd else FIELDS):
                    if turn.odd and j == 0:
                        pool.wait_ge(s_ids, nxt.group(16, 16))
                        pool.wait_ge(s_rows, nxt.group(1, 0))
                        pool.wait_ge(s_mark, nxt.group(1, 0))
                        nc.gpsimd.tensor_tensor(mark[:, 0:1], mark[:, 0:1], mark[:, 1:2], ALU.add
                                                ).then_inc(s_mark, 1)
                    gather(f)
                if PLAN[j] == "G" and has(turn, j):
                    h, s = slot(j, SPLITS, NH), slot(j, SPLITS, NL)
                    p, rows = slot(j, ALL, NP), rows_of(j)
                    pool.wait_ge(s_round, n_kind(turn, j, SPLITS) + 1)
                    was = before(turn, j, SPLITS, NL)
                    if was:
                        pool.wait_ge(s_mm, n_late(*was) + 1)
                    nc.gpsimd.tensor_tensor(low[0:rows, s, :], prod[0:rows, p, :], high[0:rows, h, :],
                                            ALU.subtract).then_inc(s_lowg, 1)

            turns(pool, emit, GROUPS - 2)

        @block.scalar
        def _(act):
            def take(turn, layer):
                z = zacc[(turn.odd + {1: 0, 0: 1, 2: 0}[layer]) % 2]
                b = bias[:, layer:layer + 1]
                if layer == 2:
                    act.wait_ge(s_mm, n_whole(turn, LAST))
                    if not turn.fixed or turn.number() > 0:
                        act.wait_ge(s_sum2, turn.count(1, 0))
                    nc.scalar.activation(direct2[:, :], z[:, :], ACT.Relu, bias=b).then_inc(s_z2, 1)
                    return
                if layer == 0:
                    act.wait_ge(s_mm, n_whole(turn, SQUARED))
                    if turn.real():
                        act.wait_ge(s_prod, turn.count(2 * N1, N1))
                        act.wait_ge(s_sum01, turn.count(1, 1))
                    to, keep, s = maps1, HALF, s_z0
                else:
                    act.wait_ge(s_mm, n_whole(turn, PAIRED))
                    if not turn.fixed or turn.number() > 0:
                        act.wait_ge(s_prod, turn.count(2 * N1, 0))
                        act.wait_ge(s_sum01, turn.count(1, 0))
                    to, keep, s = maps2, 0, s_z1
                nc.scalar.activation(to[0:HALF, :], z[0:HALF, :], ACT.Relu, bias=b[0:HALF, :])
                nc.scalar.activation(to[HALF:128, :], z[0:HALF, :], ACT.Relu, bias=b[0:HALF, :])
                nc.scalar.activation(direct01[keep:keep + HALF, :], z[HALF:128, :], ACT.Relu,
                                     bias=b[HALF:128, :]).then_inc(s, 1)

            def spread_tile(turn, t):
                nxt = turn.shift(1)
                rows = rows_of(t)
                act.wait_ge(s_side, n_side(nxt, SPREAD_X + t) + 1)
                if turn.real():
                    act.wait_ge(s_prod, n_prod(turn, N1 + N0 + t) + 1)
                nc.scalar.activation(spread[0:rows, t, :], side(nxt, SPREAD_X + t)[0:rows, :], ACT.Copy
                                     ).then_inc(s_spread, 1)

            def emit(turn, j):
                nxt, last = turn.shift(1), turn.shift(-1)
                if turn.fixed and turn.number() == -1 and j == 0:
                    act.wait_ge(s_gather, 16 * FIELDS)
                    nc.scalar.activation(rows_x[:, :, :], landed[:, :, :], ACT.Copy).then_inc(s_rows, 1)
                    act.wait_ge(s_const, 16 * 5)
                    act.wait_ge(s_prep, 1)
                    act.wait_ge(s_zero, 2)
                if PLAN[j] in SPLITS and has(turn, j):
                    h, p, rows = slot(j, SPLITS, NH), slot(j, ALL, NP), rows_of(j)
                    if j in SQUARED:
                        act.wait_ge(s_square, n_square(turn, j) + 1)
                    else:
                        act.wait_ge(s_prod, n_prod(turn, j) + 1)
                    was = before(turn, j, SPLITS, NH)
                    if was:
                        k = PLAN[was[1]]
                        act.wait_ge(s_lowv if k == "V" else s_lowg, n_kind(*was, k) + 1)
                        act.wait_ge(s_mm, n_tile(*was) + 1)
                    nc.scalar.activation(high[0:rows, h, :], prod[0:rows, p, :], ACT.Copy
                                         ).then_inc(s_round, 1)
                if nxt.real():
                    if j == 1 + LAG:
                        act.wait_ge(s_side, n_side(nxt, TURN_X) + 1)
                        nc.scalar.activation(x_split[0:FIELDS, :], side(nxt, TURN_X)[0:FIELDS, :], ACT.Copy
                                             ).then_inc(s_high, 1)
                    if j == 8 + LAG:
                        act.wait_ge(s_side, n_side(nxt, THRICE) + 1)
                        if turn.real():
                            act.wait_ge(s_square, turn.count(N0, N0))
                        nc.scalar.activation(x_thrice[:, :], side(nxt, THRICE)[0:TRIPLE, :], ACT.Copy
                                             ).then_inc(s_thrice, 1)
                    if j == N1 + N0 - 1 + LZ:
                        take(turn, 0)
                    t = j - N1 - N0 - LAG
                    if 0 <= t:
                        spread_tile(turn, t)
                if j < LAG and turn.real():
                    spread_tile(last, N1 - LAG + j)
                if j == N1 - 1 + LZ and turn.real():
                    take(turn, 1)
                if j == LZ - 1 and last.real():
                    take(last, 2)
                if j == 14 and not turn.odd and turn.shift(-2).real():
                    before_ = turn.shift(-2)
                    act.wait_ge(s_feat, before_.group(2, 2))
                    act.dma_start(kept[bass.ds(before_.group(1, 0), 1), :, :].rearrange("g p c -> p (g c)"),
                                  feat[:, :, :].rearrange("p w b -> p (w b)")).then_inc(s_kept, 16)
                if j == 40 and not turn.odd and turn.shift(2).real():
                    act.wait_ge(s_gather, turn.group(16 * FIELDS, 2 * 16 * FIELDS))
                    act.wait_ge(s_side, n_side(nxt, TURN_X) + 1)
                    nc.scalar.activation(rows_x[:, :, :], landed[:, :, :], ACT.Copy).then_inc(s_rows, 1)

            turns(act, emit)
            act.wait_ge(s_feat, 2 * GROUPS)
            act.dma_start(kept[GROUPS - 1, :, :], feat[:, :, :].rearrange("p w b -> p (w b)")).then_inc(s_kept, 16)

            act.wait_ge(s_mlp, 16 * MLP_LOADS)
            for n in range(4):
                act.wait_ge(s_dense, n + 1)
                nc.scalar.activation(m_ctx[:, n * BANK:(n + 1) * BANK], sides[n % 2][0:DENSE, 0:BANK], ACT.Copy
                                     ).then_inc(s_dense_c, 1)
            for n in range(4):
                for m in range(7):
                    act.wait_ge(s_h, 7 * n + m + 1)
                    bank = mlp_bank(n, m)
                    if m < 4:
                        nc.scalar.activation(m_h1[:, n % 2, m, :], bank, ACT.Relu, bias=m_b1[:, m:m + 1]
                                             ).then_inc(s_hc, 1)
                    elif m < 6:
                        nc.scalar.activation(m_h2[:, n % 2, m - 4, :], bank, ACT.Relu, bias=m_b2[:, m - 4:m - 3]
                                             ).then_inc(s_hc, 1)
                    else:
                        nc.scalar.activation(m_y[0:1, n * BANK:(n + 1) * BANK], bank[0:1, :], ACT.Copy
                                             ).then_inc(s_hc, 1)

        @block.vector
        def _(dve):
            nc.vector.memset(st0b[:, 0, :], 0.0).then_inc(s_zero, 1)
            nc.vector.memset(x_split[32:64, :].bitcast(f32), 0.0).then_inc(s_zero, 1)
            dve.wait_ge(s_const, 16 * 5)
            nc.vector.tensor_copy(pick[:, :], st_pick)
            dve.wait_ge(s_wload, 16 * N_WLOADS)
            nc.vector.tensor_tensor(st0a[0:TRIPLE, 0:N0 - 1, :], st0a[0:TRIPLE, 0:N0 - 1, :], st0b[0:TRIPLE, 0:N0 - 1, :],
                                    ALU.add)
            tail = rows_of(N1 + N0 - 1)
            nc.vector.tensor_tensor(st0a[0:tail, N0 - 1, :], st0a[0:tail, N0 - 1, :], st0b[0:tail, N0 - 1, :],
                                    ALU.add).then_inc(s_fold, 1)
            dve.wait_ge(s_fold, 1)
            for j in range(TILES):
                rows = rows_of(j)
                src = (st1[0:rows, j, :] if j in PAIRED else st0a[0:rows, j - N1, :] if j in SQUARED
                       else st2[0:rows, j - N1 - N0, :])
                if PLAN[j] == "F":
                    last = nc.vector.tensor_copy(w_plain[0:rows, rank(j, "F"), :], src)
                else:
                    last = nc.vector.tensor_copy(w_high[0:rows, rank(j, SPLITS), :], src)
            last.then_inc(s_fold, 1)
            dve.wait_ge(s_fold, 2)
            for j in range(TILES):
                rows = rows_of(j)
                src = (st1[0:rows, j, :] if j in PAIRED else st0a[0:rows, j - N1, :] if j in SQUARED
                       else st2[0:rows, j - N1 - N0, :])
                if PLAN[j] != "F":
                    r = rank(j, SPLITS)
                    last = nc.vector.tensor_tensor(w_low[0:rows, r, :], src, w_high[0:rows, r, :], ALU.subtract)
            if plan_r:
                last.then_inc(s_fold, 1)
                dve.wait_ge(s_fold, 3)
            nc.vector.memset(sums[:, :, :, :], 0.0).then_inc(s_prep, 1)

            def low_part(turn, j):
                h, s = slot(j, SPLITS, NH), slot(j, SPLITS, NL)
                p, rows = slot(j, ALL, NP), rows_of(j)
                dve.wait_ge(s_round, n_kind(turn, j, SPLITS) + 1)
                was = before(turn, j, SPLITS, NL)
                if was:
                    dve.wait_ge(s_mm, n_late(*was) + 1)
                nc.vector.tensor_tensor(low[0:rows, s, :], prod[0:rows, p, :], high[0:rows, h, :],
                                        ALU.subtract).then_inc(s_lowv, 1)

            def product(turn, j):
                rows = rows_of(j)
                to = prod[0:rows, slot(j, ALL, NP), :]
                was = before(turn, j, ALL, NP)
                if was:
                    k = PLAN[was[1]]
                    if k == "F":
                        dve.wait_ge(s_mm, n_tile(*was) + 1)
                    else:
                        dve.wait_ge(s_lowv if k == "V" else s_lowg, n_kind(*was, k) + 1)
                if j in SQUARED:
                    u, nxt = j - N1, turn.shift(1)
                    if u == 0:
                        dve.wait_ge(s_thrice, nxt.count(1, 1))
                    dve.wait_ge(s_side, n_side(nxt, SQUARE_X + u) + 1)
                    nc.vector.tensor_tensor(to, side(nxt, SQUARE_X + u)[0:rows, :], x_thrice[0:rows, :],
                                            ALU.mult).then_inc(s_square, 1)
                    return
                t = j if j in PAIRED else j - N1 - N0
                if j in PAIRED:
                    if t == 0:
                        dve.wait_ge(s_z0, turn.count(1, 1))
                    dve.wait_ge(s_spread, turn.count(N1, t + 1))
                elif t == 0:
                    dve.wait_ge(s_z1, turn.count(1, 1))
                maps = maps1 if j in PAIRED else maps2
                nc.vector.tensor_tensor(to, spread[0:rows, t, :], maps[0:rows, :], ALU.mult).then_inc(s_prod, 1)

            def channel_sum(turn, which):
                src, ready, done = ((direct01, s_z1, s_sum01), (direct2, s_z2, s_sum2))[which]
                dve.wait_ge(ready, turn.count(1, 1))
                if not turn.odd and (not turn.fixed or turn.number() > 0):
                    dve.wait_ge(s_feat, turn.count(1, 0))
                nc.vector.tensor_reduce(sums[:, which, turn.odd, :],
                                        src[:, :].rearrange("p (d b) -> p b d", b=ROWS), AX.X, ALU.add
                                        ).then_inc(done, 1)

            def feature(turn, which):
                dve.wait_ge((s_sum01, s_sum2)[which], turn.count(1, 1))
                if which == 0 and (not turn.fixed or turn.number() > 1):
                    dve.wait_ge(s_kept, turn.group(16, 0))
                nc.vector.tensor_tensor(feat[:, which, :],
                                        sums[:, which, 0, :], sums[:, which, 1, :], ALU.add).then_inc(s_feat, 1)

            def emit(turn, j):
                nxt, last = turn.shift(1), turn.shift(-1)
                if has(turn, j):
                    product(turn, j)
                then, i = (turn, j - SUB) if j >= SUB else (last, j - SUB + TILES)
                if PLAN[i] == "V" and has(then, i):
                    low_part(then, i)
                if nxt.real() and j == 3 + LAG:
                    dve.wait_ge(s_high, nxt.count(1, 1))
                    nc.vector.tensor_tensor(x_split[LO:SPLIT, :], side(nxt, TURN_X)[0:FIELDS, :],
                                            x_split[0:FIELDS, :], ALU.subtract).then_inc(s_low, 1)
                if turn.real() and j == N1 + LZ + 2:
                    channel_sum(turn, 0)
                if turn.real() and turn.odd and j == N1 + LZ + 4:
                    feature(turn, 0)
                if last.real() and j == LZ + 2:
                    channel_sum(last, 1)
                if last.real() and last.odd and j == LZ + 4:
                    feature(last, 1)

            turns(dve, emit)

        @block.tensor
        def _(pe):
            def contract(turn, j):
                layer = layer_of(j)
                z = zacc[(turn.odd + {1: 0, 0: 1, 2: 0}[layer]) % 2]
                rows = rows_of(j)
                of = {1: PAIRED, 0: SQUARED, 2: LAST}[layer]
                first, last = j == of[0], j == of[-1] and tail(of) is None
                if first and layer == 1:
                    pe.wait_ge(s_z0, turn.count(1, 1))
                    if not turn.fixed or turn.number() > 0:
                        pe.wait_ge(s_z1, turn.count(1, 0))
                if first and layer == 0 and turn.real():
                    if not turn.fixed or turn.number() > 0:
                        pe.wait_ge(s_z2, turn.count(1, 0))
                if first and layer == 2:
                    pe.wait_ge(s_z1, turn.count(1, 1))

                def mm(hf, w, x, start, stop):
                    return nc.tensor.matmul(z[:, hf * BANK:(hf + 1) * BANK], w, x[:, hf * BANK:(hf + 1) * BANK],
                                            start=start, stop=stop)
                if PLAN[j] == "F":
                    if j in SQUARED:
                        pe.wait_ge(s_square, n_square(turn, j) + 1)
                    else:
                        pe.wait_ge(s_prod, n_prod(turn, j) + 1)
                    x = prod[0:rows, slot(j, ALL, NP), :]
                    for hf in range(2):
                        done = mm(hf, w_plain[0:rows, rank(j, "F"), :], x, first, last)
                else:
                    h, r = slot(j, SPLITS, NH), rank(j, SPLITS)
                    pe.wait_ge(s_round, n_kind(turn, j, SPLITS) + 1)
                    for hf in range(2):
                        mm(hf, w_low[0:rows, r, :], high[0:rows, h, :], first, False)
                    for hf in range(2):
                        done = mm(hf, w_high[0:rows, r, :], high[0:rows, h, :], False, False)
                return done

            def contract_low(turn, j):
                layer, rows, k = layer_of(j), rows_of(j), PLAN[j]
                z = zacc[(turn.odd + {1: 0, 0: 1, 2: 0}[layer]) % 2]
                s, r = slot(j, SPLITS, NL), rank(j, SPLITS)
                last = j == tail({1: PAIRED, 0: SQUARED, 2: LAST}[layer])
                pe.wait_ge(s_lowv if k == "V" else s_lowg, n_kind(turn, j, k) + 1)
                for hf in range(2):
                    cols = slice(hf * BANK, (hf + 1) * BANK)
                    done = nc.tensor.matmul(z[:, cols], w_high[0:rows, r, :], low[0:rows, s, cols],
                                            start=False, stop=last)
                return done

            def side_work(turn, j):
                nxt = turn.shift(1)
                if not nxt.real():
                    return

                def pick_fields(use, first, n):
                    for hf in range(2):
                        cols = slice(hf * BANK, (hf + 1) * BANK)
                        done = nc.tensor.matmul(side(nxt, use)[0:n, cols], pick[:, first:first + n],
                                                x_split[:, cols], start=True, stop=True)
                    done.then_inc(s_side, 1)

                if j == 1:
                    pe.wait_ge(s_rows, nxt.group(1, 1))
                    if turn.real():
                        pe.wait_ge(s_spread, turn.count(N1, N1 - 1))
                    for d in range(CHAN):
                        done = nc.tensor.matmul(side(nxt, TURN_X)[0:FIELDS, d * ROWS:(d + 1) * ROWS],
                                                rows_x[:, :, nxt.odd * CHAN + d], ident[:, :],
                                                start=d * ROWS % BANK == 0, stop=(d + 1) * ROWS % BANK == 0,
                                                skip_group_check=True)
                    done.then_inc(s_side, 1)
                if j == 8:
                    pe.wait_ge(s_low, nxt.count(1, 1))
                    if turn.real():
                        pe.wait_ge(s_spread, turn.count(N1, N1))
                    pick_fields(THRICE, BACK, TRIPLE)
                u = j - N1 + AHEAD
                if 0 <= u < N0:
                    if u == 1:
                        pe.wait_ge(s_thrice, nxt.count(1, 1))
                    elif u > 1:
                        pe.wait_ge(s_square, nxt.count(N0, u - 1))
                    pick_fields(SQUARE_X + u, PERIODIC + PER0 * u, TRIPLE)
                t = j - N1 - N0
                if 0 <= t:
                    if t < 2:
                        pe.wait_ge(s_square, nxt.count(N0, N0 - 1 + t))
                    else:
                        pe.wait_ge(s_spread, nxt.count(N1, t - 1))
                    pick_fields(SPREAD_X + t, t * MAPS, MAPS)

            def emit(turn, j):
                if turn.fixed and turn.number() == -1 and j == 0:
                    pe.wait_ge(s_const, 16 * 5)
                    pe.wait_ge(s_prep, 1)
                if has(turn, j):
                    done = contract(turn, j)
                    then = step_back(turn, j, LATE)
                    if then and PLAN[then[1]] in SPLITS:
                        done = contract_low(*then)
                    done.then_inc(s_mm, 1)
                if turn.fixed and (turn.number(), j) in (
                        (-1, SQUARED[-1]), (CHUNKS - 1, PAIRED[-1]), (CHUNKS - 1, TILES - 1)):
                    for i in range(j - LATE + 1, j + 1):
                        if PLAN[i] in SPLITS:
                            done = contract_low(turn, i)
                        else:
                            done = nc.tensor.matmul(zacc[1 if j in SQUARED else 0][0:1, 0:1], ident[0:1, 0:1], ident[0:1, 0:1],
                                                    start=True, stop=True)
                        done.then_inc(s_mm, 1)
                side_work(turn, j)

            turns(pe, emit)

            pe.wait_ge(s_mlp, 16 * MLP_LOADS)
            for n in range(4):
                if n >= 2:
                    pe.wait_ge(s_dense_c, n - 1)
                for g in range(4):
                    done = nc.tensor.matmul(sides[n % 2][0:DENSE, g * ROWS:(g + 1) * ROWS], m_dense[:, 4 * n + g, :],
                                            ident[:, :], start=g == 0, stop=g == 3, skip_group_check=True)
                done.then_inc(s_dense, 1)
            pe.wait_ge(s_z2, CHUNKS)
            for n in range(4):
                cols = slice(n * BANK, (n + 1) * BANK)
                x = m_feats[:, n * BANK // ROWS:(n + 1) * BANK // ROWS, :, :]
                for m in range(7):
                    k = 7 * n + m
                    if m == 0:
                        pe.wait_ge(s_dense_c, n + 1)
                        pe.wait_ge(s_feats[n], 16)
                    if m in (4, 6):
                        pe.wait_ge(s_hc, k)
                    elif k >= 4:
                        pe.wait_ge(s_hc, k - 3)
                    bank = mlp_bank(n, m)
                    if m < 4:
                        ms = slice(m * 128, (m + 1) * 128)
                        nc.tensor.matmul(bank, m_w1[:, 0, ms], x[:, :, 0, :], start=True, stop=False)
                        nc.tensor.matmul(bank, m_w1[:, 1, ms], x[:, :, 1, :], start=False, stop=False)
                        done = nc.tensor.matmul(bank, m_w1d[:, ms], m_ctx[:, cols], start=False, stop=True)
                    elif m < 6:
                        ms = slice((m - 4) * 128, (m - 3) * 128)
                        for q in range(4):
                            done = nc.tensor.matmul(bank, m_w2[:, q, ms], m_h1[:, n % 2, q, :],
                                                    start=q == 0, stop=q == 3)
                    else:
                        for q in range(2):
                            done = nc.tensor.matmul(bank[0:1, :], m_w3[:, q:q + 1], m_h2[:, n % 2, q, :],
                                                    start=q == 0, stop=q == 1)
                    done.then_inc(s_h, 1)


MLP_LOADS = 9


def w0_runs():
    runs = []
    for j in range(SHIFTS):
        u, s = divmod(j, PER0)
        cuts = sorted({0, s, FIELDS - PER0 * u, FIELDS})
        runs += [(u, s, lo, hi) for lo, hi in zip(cuts, cuts[1:])]
    return runs


W0_RUNS = w0_runs()
N_WLOADS = 4 + 2 * len(W0_RUNS) - sum(u == s == 0 for u, s, _, _ in W0_RUNS)


def selections():
    pick = np.zeros((SPLIT, PICK_W), np.float32)
    for at in (0, LO):
        for f in range(FIELDS):
            pick[at + f, f * HALF:(f + 1) * HALF] = 1.0
            pick[at + f, PERIODIC + f:BACK:FIELDS] = 1.0
            for s in range(PER0):
                pick[at + f, BACK + s * FIELDS + (f + s) % FIELDS] = 1.0
    return pick


def kernel(**inputs):
    import concourse.bacc as _bacc
    from concourse.bass_utils import run_bass_kernel_spmd as _run

    nc = _bacc.Bacc("TRN2", target_bir_lowering=False, num_devices=1)
    arrays, args = {}, {}
    given = {name: np.ascontiguousarray(x) for name, x in inputs.items()}
    given["pick"] = selections()
    given["ident"] = np.eye(128, dtype=np.float32)
    for name, x in given.items():
        arrays[f"in_{name}"] = x
        args[name] = nc.dram_tensor(f"in_{name}", x.shape, mybir.dt.from_np(x.dtype), kind="ExternalInput").ap()
    out = nc.dram_tensor("out", (BATCH, 1), mybir.dt.float32, kind="ExternalOutput").ap()
    build(nc, args, out)
    return _run(nc, [arrays], core_ids=[0]).results[0]["out"]
```

```python
import numpy as np
import concourse.bass as bass
from concourse import mybir
from concourse.alu_op_type import AluOpType as ALU
from contextlib import ExitStack

BATCH, FIELDS, DIM = 2048, 39, 16
MAPS = 128
HALF = MAPS // 2
ROWS = 128
GROUPS = BATCH // ROWS
CHAN = DIM // 2
COLS = ROWS * CHAN
BANK = 512
CHUNKS = 2 * GROUPS
SHIFTS = FIELDS // 2 + 1
PER0 = 3
N0 = -(-SHIFTS // PER0)
N1 = -(-FIELDS // 2)
TILES = N1 + N0 + N1
SPLIT = 2 * FIELDS
TRIPLE = FIELDS * PER0
PERIODIC = N1 * MAPS
BACK = PERIODIC + TRIPLE + PER0 * (N0 - 1)
PICK_W = BACK + TRIPLE
D1, D2, D3, DENSE = 272, 512, 256, 16
CTX = 64 + DENSE
PAIRED = range(0, N1)
SQUARED = range(N1, N1 + N0)
LAST = range(N1 + N0, TILES)

PLAN = "FVFVFVFFVFVFFVFVFVFVFVFFFVFVFVFVFVVFVFVVFVFVFVV"
NP, NH = 8, 3
LATE = 2
LZ = 4
LAG = 2
SUB = 3
AHEAD = 4
LOW_ROWS_AT, COPY_ROWS_AT = 42, 40
KEEP_AT = 14
TURN_AT, THRICE_AT = 3, 9
OFFSET = 12


def layer_of(j):
    return 1 if j in PAIRED else 0 if j in SQUARED else 2


def rows_of(j):
    if j in SQUARED:
        u = j - N1
        return FIELDS * min(PER0, SHIFTS - PER0 * u)
    t = j if j in PAIRED else j - N1 - N0
    return HALF * min(2, FIELDS - 2 * t)


def stacked(j):
    return PLAN[j] == "V" and rows_of(j) == HALF


def rank(j, kinds):
    return sum(PLAN[i] in kinds for i in range(j))


def slot(j, kinds, ring):
    short = -rank(TILES, kinds) % ring
    whole = rank(TILES, kinds) - short * (ring - 1)
    assert whole >= 0
    r = rank(j, kinds)
    return r % ring if r < whole else (r - whole) % (ring - 1)


def earlier(j, kinds, ring):
    for back, upto in ((0, j), (1, TILES)):
        for i in reversed(range(upto)):
            if PLAN[i] in kinds and slot(i, kinds, ring) == slot(j, kinds, ring):
                return back, i


class Turn:

    def __init__(self, loop, plus):
        self.loop, self.plus = loop, plus
        self.fixed, self.odd = loop is None, plus % 2

    def shift(self, n):
        return Turn(self.loop, self.plus + n)

    def number(self):
        return self.plus

    def real(self):
        return not self.fixed or 0 <= self.plus < CHUNKS

    def count(self, per, plus):
        return self.linear(2 * per, per * self.plus + plus)

    def group(self, per, plus):
        return self.linear(per, per * (self.plus // 2) + plus)

    def linear(self, per, plus):
        return plus if self.fixed else self.loop * per + plus


def turns(engine, emit, loops=GROUPS - 1):
    for j in range(TILES):
        emit(Turn(None, -1), j)
    for p in range(2 * TILES + OFFSET):
        emit(Turn(None, p // TILES), p % TILES)
    with engine.Fori(1, loops) as g:
        for p in range(OFFSET, OFFSET + 2 * TILES):
            emit(Turn(g, p // TILES), p % TILES)
    for p in range(2 * loops * TILES + OFFSET, CHUNKS * TILES + OFFSET):
        emit(Turn(None, p // TILES), p % TILES)


def build(nc, a, out):
    f32, f32r, i32 = mybir.dt.float32, mybir.dt.float32r, mybir.dt.int32
    ACT, AX = mybir.ActivationFunctionType, mybir.AxisListType
    ALL = "FV"
    plan_f, plan_r = PLAN.count("F"), PLAN.count("V")

    kept = nc.dram_tensor("features", (GROUPS, 128, 2 * ROWS), f32, kind="Internal").ap()

    ctx = ExitStack()
    with ctx:
        def sb(name, shape, dt=f32):
            return ctx.enter_context(nc.sbuf_tensor(name, shape, dt))

        def ps(name, banks):
            return ctx.enter_context(nc.psum_tensor(name, [128, banks * BANK], f32))

        def sem(name):
            return ctx.enter_context(nc.semaphore(name))

        with nc.sbuf_tensor("spread_r", [128, N1, COLS], f32r) as spread_r:
            pass
        spread = sb("spread", [128, N1, COLS])
        w_plain = sb("w_plain", [128, plan_f, MAPS])
        w_high = sb("w_high", [128, plan_r, MAPS], f32r)
        w_low = sb("w_low", [128, plan_r, MAPS], f32r)
        pick = sb("pick", [SPLIT, PICK_W], f32r)
        ident_r = sb("ident_r", [128, 128], f32r)
        bias = sb("bias", [128, 3])
        mark = sb("mark", [128, 2])
        rows_id = sb("rows_id", [ROWS, FIELDS], i32)
        landed = sb("landed", [ROWS, FIELDS, DIM])
        rows_split = sb("rows_split", [ROWS, DIM, SPLIT], f32r)
        x_split = sb("x_split", [SPLIT, COLS], f32r)
        x_thrice = sb("x_thrice", [TRIPLE, COLS])
        maps1 = sb("maps1", [128, COLS])
        maps2 = sb("maps2", [128, COLS])
        direct01 = sb("direct01", [128, COLS])
        direct2 = sb("direct2", [128, COLS])
        sums = sb("sums", [128, 2, 2, ROWS])
        feat = sb("feat", [128, 2, ROWS])
        with nc.sbuf_tensor("low", [128, NP, COLS], f32r) as low:
            pass
        prod = sb("prod", [128, NP, COLS])
        high = sb("high", [128, NH, COLS], f32r)

        zacc = [ps("zacc_a", 2), ps("zacc_b", 2)]
        sides = [ps("side_a", 2), ps("side_b", 2)]

        s_const = sem("s_const")
        s_wload12 = sem("s_wload12")
        s_wload = sem("s_wload")
        s_zero = sem("s_zero")
        s_pick = sem("s_pick")
        s_prep = sem("s_prep")
        s_fold = sem("s_fold")
        s_ids = sem("s_ids")
        s_mark = sem("s_mark")
        s_gather = sem("s_gather")
        s_rowh = sem("s_rowh")
        s_rows = sem("s_rows")
        s_side = sem("s_side")
        s_x = sem("s_x")
        s_thrice = sem("s_thrice")
        s_spread = sem("s_spread")
        s_prod = sem("s_prod")
        s_square = sem("s_square")
        s_round = sem("s_round")
        s_lowv = sem("s_lowv")
        s_mm = sem("s_mm")
        s_z0 = sem("s_z0")
        s_z1 = sem("s_z1")
        s_z2 = sem("s_z2")
        s_sum01 = sem("s_sum01")
        s_sum2 = sem("s_sum2")
        s_feat = sem("s_feat")
        s_kept = sem("s_kept")
        s_feats = [sem(f"s_feats{n}") for n in range(4)]
        s_mlp = sem("s_mlp")
        s_dense = sem("s_dense")
        s_dense_c = sem("s_dense_c")
        s_ctx = sem("s_ctx")
        s_gaps = sem("s_gaps")
        s_top = sem("s_top")
        s_fh = sem("s_fh")
        s_fl = sem("s_fl")
        s_h1h = sem("s_h1h")
        s_h1l = sem("s_h1l")
        s_h = sem("s_h")
        s_hc = sem("s_hc")
        s_out = sem("s_out")

        def n_kind(turn, j, kinds):
            at_start = sum(PLAN[i] in kinds for i in SQUARED)
            if turn.fixed and turn.number() < 0:
                return rank(j, kinds) - rank(N1, kinds)
            if turn.fixed and turn.number() == CHUNKS - 1 and j in LAST:
                return turn.count(rank(TILES, kinds), rank(j, kinds))
            return turn.count(rank(TILES, kinds), at_start + rank(j, kinds))

        def n_tile(turn, j, plus=0):
            if turn.fixed and turn.number() < 0:
                return j - N1 + plus
            missing = N0 - LATE if turn.fixed and turn.number() == CHUNKS - 1 and j in LAST else 0
            return turn.count(TILES, N0 + LATE + j - missing + plus)

        def n_late(turn, j):
            return n_tile(turn, j, LATE)

        def tail(of):
            split = [j for j in of if PLAN[j] == "V"]
            return split[-1] if split and split[-1] + LATE >= of[-1] else None

        def n_whole(turn, of):
            end = tail(of)
            extra = 1 + (0 if end is None else end + LATE - of[-1])
            return n_tile(turn, of[-1], extra)

        def step_back(turn, j, n):
            for _ in range(n):
                j -= 1
                if j < 0:
                    turn, j = turn.shift(-1), TILES - 1
                    if turn.fixed and turn.number() < 0:
                        return None
                if not has(turn, j):
                    return None
            return turn, j

        def n_prod(turn, j):
            return turn.count(2 * N1, j if j in PAIRED else j - N0)

        def n_square(turn, j):
            return turn.shift(1).count(N0, j - N1)

        def n_side(turn, use):
            return turn.count(SIDES, use)

        TURN_X, THRICE, SQUARE_X, SPREAD_X = 0, 1, 2, 2 + N0
        SIDES = SPREAD_X + N1

        def side(turn, use):
            return sides[(turn.plus * SIDES + use) % 2]

        def has(turn, j):
            if j in SQUARED:
                return turn.shift(1).real()
            return turn.real()

        def before(turn, j, kinds, ring):
            back, i = earlier(j, kinds, ring)
            then = turn.shift(-back) if back else turn
            if then.fixed and not has(then, i):
                return before(then, i, kinds, ring) if then.number() >= 0 or i in LAST else None
            return then, i

        staged = spread[:, :, :].rearrange("p t c -> p (t c)")
        st0a = staged[:, 0:N0 * MAPS].rearrange("p (t s) -> p t s", s=MAPS)
        st0b = staged[:, N0 * MAPS:2 * N0 * MAPS].rearrange("p (t s) -> p t s", s=MAPS)
        st1 = staged[:, 2 * N0 * MAPS:(2 * N0 + N1) * MAPS].rearrange("p (t s) -> p t s", s=MAPS)
        st2 = staged[:, (2 * N0 + N1) * MAPS:(2 * N0 + 2 * N1) * MAPS].rearrange("p (t s) -> p t s", s=MAPS)
        st_pick = staged[0:SPLIT, 8192:8192 + PICK_W]
        st_ident = staged[:, 8192 + PICK_W:8192 + PICK_W + 128]
        at = [0]
        staged_r = spread_r[:, :, :].rearrange("p t c -> p (t c)")

        def mlp(parts, n):
            at[0] += n
            assert at[0] <= N1 * COLS
            return staged[0:parts, at[0] - n:at[0]], staged_r[0:parts, at[0] - n:at[0]]

        def cut(views, shape):
            return [v.rearrange("p (t n) -> p t n", t=shape) for v in views]

        m_w1, m_w1l = cut(mlp(128, 2 * D2), 2)
        m_w1h = cut(mlp(128, 2 * D2), 2)[1]
        m_w2, m_w2l = cut(mlp(128, 4 * D3), 4)
        m_w2h = cut(mlp(128, 4 * D3), 4)[1]
        m_w1d = mlp(DENSE, D2)[0]
        m_wc = mlp(CTX, D2)[1]
        m_ctx = mlp(CTX, BATCH)[1]
        m_w3, m_b1, m_b2, m_ident = mlp(128, 2)[0], mlp(128, 4)[0], mlp(128, 2)[0], mlp(128, 128)[0]
        m_dense = mlp(128, GROUPS * DENSE)[0].rearrange("p (g e) -> p g e", e=DENSE)
        m_feats, m_fl = [v.rearrange("p (g w b) -> p g w b", g=GROUPS, w=2) for v in mlp(128, GROUPS * 2 * ROWS)]
        m_fh = mlp(128, GROUPS * 2 * ROWS)[1].rearrange("p (g w b) -> p g w b", g=GROUPS, w=2)
        m_h1h = cut(mlp(128, 2 * 4 * BANK), 8)[1]
        m_h1, m_h1l = [v[:, 0:4, :].rearrange("p s (h c) -> p (s h) c", c=BANK) for v in (prod, low)]
        m_h2 = prod[:, 4:6, :].rearrange("p s (h c) -> p (s h) c", c=BANK)
        m_y = prod[0:1, 6:8, :].rearrange("p s c -> p (s c)")

        def mlp_bank(k):
            return zacc[k % 4 // 2][:, k % 2 * BANK:(k % 2 + 1) * BANK]

        w0, w1, w2 = a["L0_rec_w0"], a["L0_rec_w1"], a["L0_rec_w2"]
        PER = BANK // ROWS
        FULL = N1 - 1
        block = ctx.enter_context(nc.Block())

        def w0_run(start, n):
            return w0.rearrange("h k s -> (h k) s")[start:start + (n - 1) * (FIELDS + 1) + 1:FIELDS + 1, :]

        @block.sync
        def _(sp):
            ids = a["ids"]
            sp.dma_start(rows_id[:, :], ids[0:ROWS, :]).then_inc(s_ids, 16)
            sp.dma_start(st_pick, a["pick"]).then_inc(s_const, 16)
            sp.dma_start(st_ident, a["ident"]).then_inc(s_const, 16)
            for n, b in enumerate(("L0_rec_b0", "L0_rec_b1", "L0_rec_b2")):
                sp.dma_start(bias[:, n:n + 1], a[b].rearrange("(p o) -> p o", o=1)).then_inc(s_const, 16)
            for w, st in ((w1, st1), (w2, st2)):
                flat = w.rearrange("h k s -> (h k) s")
                sp.dma_start(st[:, 0:FULL, :], flat[0:FULL * 128, :].rearrange("(t p) s -> p t s", p=128)
                             ).then_inc(s_wload12, 16)
                sp.dma_start(st[0:HALF, FULL, :], flat[FULL * 128:, :]).then_inc(s_wload12, 16)
            for u, s, lo, hi in W0_RUNS:
                f, g = (lo - s) % FIELDS, (lo + PER0 * u) % FIELDS
                sp.dma_start(st0a[s * FIELDS + lo:s * FIELDS + hi, u, :], w0_run(f * FIELDS + g, hi - lo)
                             ).then_inc(s_wload, 16)
            with sp.Fori(1, GROUPS) as g:
                sp.wait_ge(s_gather, g * (16 * FIELDS))
                sp.dma_start(rows_id[:, :], ids[bass.ds(g * ROWS, ROWS), :]).then_inc(s_ids, 16)
            sp.wait_ge(s_prod, 2 * N1 * CHUNKS)
            wt1, wt2 = a["W_top1"], a["W_top2"]
            loads = [
                (m_w1[0:HALF, 0, :], wt1[HALF:2 * HALF, :]), (m_w1[HALF:128, 0, :], wt1[0:HALF, :]),
                (m_w1[:, 1, :], wt1[MAPS:2 * MAPS, :]), (m_w1d, wt1[2 * MAPS:D1, :]),
                (m_w2, wt2.rearrange("(t p) n -> p t n", p=128)),
                (m_w3, a["W_top3"].rearrange("(t p) o -> p (t o)", p=128)),
                (m_b1, a["b_top1"].rearrange("(t p) -> p t", p=128)),
                (m_b2, a["b_top2"].rearrange("(t p) -> p t", p=128)),
                (m_ident, a["ident"]),
                (m_dense, a["dense_ctx"].rearrange("(g p) e -> p g e", p=128)),
            ]
            assert len(loads) == MLP_LOADS
            for dst, src in loads:
                sp.dma_start(dst, src, allow_slow_non_contiguous=True).then_inc(s_mlp, 16)
            for n in range(4):
                sp.wait_ge(s_kept, 16 * PER * (n + 1))
                sp.dma_start(m_feats[:, PER * n:PER * (n + 1), :, :].rearrange("p g w b -> p g (w b)"),
                             kept[PER * n:PER * (n + 1), :, :].rearrange("g p c -> p g c")).then_inc(s_feats[n], 16)
            sp.wait_ge(s_hc, 28)
            sp.dma_start(out.rearrange("b o -> o b"), m_y[0:1, :]).then_inc(s_out, 16)
            sp.wait_ge(s_out, 16)

        @block.gpsimd
        def _(pool):
            tables = [a[f"tbl_{f}"] for f in range(FIELDS)]

            nc.gpsimd.memset(mark[:, :], 0.0).then_inc(s_mark, 1)

            def gather(f):
                nc.gpsimd.indirect_dma_start(
                    out=landed[:, f, :], out_offset=None, in_=tables[f],
                    in_offset=bass.IndirectOffsetOnAxis(ap=rows_id[:, f:f + 1], axis=0),
                ).then_inc(s_gather, 16)

            def emit(turn, j):
                if turn.fixed and turn.number() == -1 and j == 0:
                    pool.wait_ge(s_ids, 16)
                    for f in range(FIELDS):
                        gather(f)
                nxt = turn.shift(3 if turn.odd else 2)
                half = FIELDS // 2 + 1
                f = j if turn.odd else half + j
                if nxt.real() and f < (half if turn.odd else FIELDS):
                    if turn.odd and j == 0:
                        pool.wait_ge(s_ids, nxt.group(16, 16))
                        pool.wait_ge(s_rows, nxt.group(1, 0))
                        pool.wait_ge(s_mark, nxt.group(1, 0))
                        nc.gpsimd.tensor_tensor(mark[:, 0:1], mark[:, 0:1], mark[:, 1:2], ALU.add
                                                ).then_inc(s_mark, 1)
                    gather(f)

            turns(pool, emit, GROUPS - 2)

        @block.scalar
        def _(act):
            act.wait_ge(s_zero, 1)
            for u, s, lo, hi in W0_RUNS:
                if (u, s) != (0, 0):
                    f, g = (lo - s) % FIELDS, (lo + PER0 * u) % FIELDS
                    act.dma_start(st0b[s * FIELDS + lo:s * FIELDS + hi, u, :], w0_run(g * FIELDS + f, hi - lo)
                                  ).then_inc(s_wload, 16)

            def take(turn, layer):
                z = zacc[(turn.odd + {1: 0, 0: 1, 2: 0}[layer]) % 2]
                b = bias[:, layer:layer + 1]
                if layer == 2:
                    act.wait_ge(s_mm, n_whole(turn, LAST))
                    if not turn.fixed or turn.number() > 0:
                        act.wait_ge(s_sum2, turn.count(1, 0))
                    nc.scalar.activation(direct2[:, :], z[:, :], ACT.Relu, bias=b).then_inc(s_z2, 1)
                    return
                if layer == 0:
                    act.wait_ge(s_mm, n_whole(turn, SQUARED))
                    if turn.real():
                        act.wait_ge(s_prod, turn.count(2 * N1, N1))
                        act.wait_ge(s_sum01, turn.count(1, 1))
                    to, keep, s = maps1, HALF, s_z0
                else:
                    act.wait_ge(s_mm, n_whole(turn, PAIRED))
                    if not turn.fixed or turn.number() > 0:
                        act.wait_ge(s_prod, turn.count(2 * N1, 0))
                        act.wait_ge(s_sum01, turn.count(1, 0))
                    to, keep, s = maps2, 0, s_z1
                nc.scalar.activation(to[0:HALF, :], z[0:HALF, :], ACT.Relu, bias=b[0:HALF, :])
                nc.scalar.activation(to[HALF:128, :], z[0:HALF, :], ACT.Relu, bias=b[0:HALF, :])
                nc.scalar.activation(direct01[keep:keep + HALF, :], z[HALF:128, :], ACT.Relu,
                                     bias=b[HALF:128, :]).then_inc(s, 1)

            def high_rows():
                nc.scalar.activation(rows_split[:, :, 0:FIELDS].rearrange("p d f -> p f d"), landed[:, :, :], ACT.Copy
                                     ).then_inc(s_rowh, 1)

            def spread_tile(turn, t):
                nxt = turn.shift(1)
                rows = rows_of(t)
                if turn.fixed and turn.number() == -1 and t == 0:
                    act.wait_ge(s_prep, 1)
                act.wait_ge(s_side, n_side(nxt, SPREAD_X + t) + 1)
                if turn.real():
                    act.wait_ge(s_prod, n_prod(turn, N1 + N0 + t) + 1)
                nc.scalar.activation(spread[0:rows, t, :], side(nxt, SPREAD_X + t)[0:rows, :], ACT.Copy
                                     ).then_inc(s_spread, 1)

            def emit(turn, j):
                nxt, last = turn.shift(1), turn.shift(-1)
                if turn.fixed and turn.number() == -1 and j == 0:
                    act.wait_ge(s_gather, 16 * FIELDS)
                    high_rows()
                    act.wait_ge(s_const, 16 * 5)
                if PLAN[j] == "V" and has(turn, j):
                    h, p, rows = slot(j, "V", NH), slot(j, ALL, NP), rows_of(j)
                    if j in SQUARED:
                        act.wait_ge(s_square, n_square(turn, j) + 1)
                    else:
                        act.wait_ge(s_prod, n_prod(turn, j) + 1)
                    was = before(turn, j, "V", NH)
                    if was:
                        act.wait_ge(s_lowv, n_kind(*was, "V") + 1)
                        act.wait_ge(s_mm, (n_late if stacked(was[1]) else n_tile)(*was) + 1)
                    nc.scalar.activation(high[0:rows, h, :], prod[0:rows, p, :], ACT.Copy
                                         ).then_inc(s_round, 1)
                if nxt.real():
                    if j == TURN_AT + LAG:
                        act.wait_ge(s_side, n_side(nxt, TURN_X) + 1)
                        nc.scalar.activation(x_split[:, :], side(nxt, TURN_X)[0:SPLIT, :], ACT.Copy
                                             ).then_inc(s_x, 1)
                    if j == THRICE_AT + LAG:
                        act.wait_ge(s_side, n_side(nxt, THRICE) + 1)
                        if turn.real():
                            act.wait_ge(s_square, turn.count(N0, N0))
                        nc.scalar.activation(x_thrice[:, :], side(nxt, THRICE)[0:TRIPLE, :], ACT.Copy
                                             ).then_inc(s_thrice, 1)
                    if j == N1 + N0 - 1 + LZ:
                        take(turn, 0)
                    t = j - N1 - N0 - LAG
                    if 0 <= t:
                        spread_tile(turn, t)
                if j < LAG and turn.real():
                    spread_tile(last, N1 - LAG + j)
                if j == N1 - 1 + LZ and turn.real():
                    take(turn, 1)
                if j == LZ - 1 and last.real():
                    take(last, 2)
                if j == KEEP_AT and not turn.odd and turn.shift(-2).real():
                    done = turn.shift(-2)
                    act.wait_ge(s_feat, done.group(2, 2))
                    act.dma_start(kept[bass.ds(done.group(1, 0), 1), :, :].rearrange("g p c -> p (g c)"),
                                  feat[:, :, :].rearrange("p w b -> p (w b)")).then_inc(s_kept, 16)
                if j == COPY_ROWS_AT and not turn.odd and turn.shift(2).real():
                    act.wait_ge(s_gather, turn.group(16 * FIELDS, 2 * 16 * FIELDS))
                    act.wait_ge(s_side, n_side(nxt, TURN_X) + 1)
                    high_rows()

            turns(act, emit)
            act.wait_ge(s_feat, 2 * GROUPS)
            act.dma_start(kept[GROUPS - 1, :, :], feat[:, :, :].rearrange("p w b -> p (w b)")).then_inc(s_kept, 16)

            act.wait_ge(s_mlp, 16 * MLP_LOADS)
            act.wait_ge(s_gaps, 1)
            for i in range(2):
                act.wait_ge(s_dense, i + 1)
                for place in (0, 32):
                    last = nc.scalar.activation(m_ctx[place:place + DENSE, i * COLS:(i + 1) * COLS],
                                                sides[i][0:DENSE, :], ACT.Copy)
                last.then_inc(s_dense_c, 1)

            def high_features(n):
                act.wait_ge(s_feats[n], 16)
                nc.scalar.activation(m_fh[:, PER * n:PER * (n + 1), :, :], m_feats[:, PER * n:PER * (n + 1), :, :],
                                     ACT.Copy).then_inc(s_fh, 1)

            high_features(0)
            for k, (layer, n, m) in enumerate(MLP_STEPS):
                act.wait_ge(s_h, k + 1)
                bank = mlp_bank(k)
                if layer == 1:
                    i = n % 2 * 4 + m
                    nc.scalar.activation(m_h1[:, i, :], bank, ACT.Relu, bias=m_b1[:, m:m + 1]).then_inc(s_hc, 1)
                    act.wait_ge(s_hc, k + 1)
                    nc.scalar.activation(m_h1h[:, i, :], m_h1[:, i, :], ACT.Copy).then_inc(s_h1h, 1)
                    if m == 0 and n < 3:
                        high_features(n + 1)
                elif layer == 2:
                    nc.scalar.activation(m_h2[:, n % 2 * 2 + m, :], bank, ACT.Relu, bias=m_b2[:, m:m + 1]
                                         ).then_inc(s_hc, 1)
                else:
                    nc.scalar.activation(m_y[0:1, n * BANK:(n + 1) * BANK], bank[0:1, :], ACT.Copy
                                         ).then_inc(s_hc, 1)

        @block.vector
        def _(dve):
            nc.vector.memset(st0b[:, 0, :], 0.0).then_inc(s_zero, 1)
            dve.wait_ge(s_const, 16 * 5)
            nc.vector.tensor_copy(ident_r[:, :], st_ident)
            nc.vector.tensor_copy(pick[:, :], st_pick).then_inc(s_pick, 1)

            def low_rows(n):
                dve.wait_ge(s_rowh, n)
                nc.vector.tensor_tensor(rows_split[:, :, FIELDS:SPLIT].rearrange("p d f -> p f d"), landed[:, :, :],
                                        rows_split[:, :, 0:FIELDS].rearrange("p d f -> p f d").bitcast(f32),
                                        ALU.subtract).then_inc(s_rows, 1)


            def staged_tile(j):
                rows = rows_of(j)
                return (st1[0:rows, j, :] if j in PAIRED else st0a[0:rows, j - N1, :] if j in SQUARED
                        else st2[0:rows, j - N1 - N0, :])

            def prepare(tiles, step):
                split = [j for j in tiles if PLAN[j] != "F"]
                for j in tiles:
                    if PLAN[j] == "F":
                        nc.vector.tensor_copy(w_plain[0:rows_of(j), rank(j, "F"), :], staged_tile(j))
                for j in split:
                    if stacked(j):
                        nc.vector.tensor_copy(w_high[HALF:128, rank(j, "V"), :], staged_tile(j))
                    last = nc.vector.tensor_copy(w_high[0:rows_of(j), rank(j, "V"), :], staged_tile(j))
                if split:
                    last.then_inc(s_fold, 1)
                    dve.wait_ge(s_fold, step)
                for j in split:
                    nc.vector.tensor_tensor(w_low[0:rows_of(j), rank(j, "V"), :], staged_tile(j),
                                            w_high[0:rows_of(j), rank(j, "V"), :], ALU.subtract)

            dve.wait_ge(s_wload12, 16 * 4)
            prepare([*PAIRED, *LAST], 1)
            low_rows(1)
            dve.wait_ge(s_wload, 16 * N_WLOADS)
            nc.vector.tensor_tensor(st0a[0:TRIPLE, 0:N0 - 1, :], st0a[0:TRIPLE, 0:N0 - 1, :], st0b[0:TRIPLE, 0:N0 - 1, :],
                                    ALU.add)
            fewer = rows_of(N1 + N0 - 1)
            nc.vector.tensor_tensor(st0a[0:fewer, N0 - 1, :], st0a[0:fewer, N0 - 1, :], st0b[0:fewer, N0 - 1, :],
                                    ALU.add).then_inc(s_fold, 1)
            dve.wait_ge(s_fold, 2)
            prepare(SQUARED, 3)
            nc.vector.memset(sums[:, :, :, :], 0.0).then_inc(s_prep, 1)

            def low_part(turn, j):
                rows = rows_of(j)
                whole, top = prod[0:rows, slot(j, ALL, NP), :], high[0:rows, slot(j, "V", NH), :]
                dve.wait_ge(s_round, n_kind(turn, j, "V") + 1)
                to = high[HALF:128, slot(j, "V", NH), :] if stacked(j) else low[0:rows, slot(j, ALL, NP), :]
                nc.vector.tensor_tensor(to, whole, top, ALU.subtract).then_inc(s_lowv, 1)

            def product(turn, j):
                rows = rows_of(j)
                to = prod[0:rows, slot(j, ALL, NP), :]
                was = before(turn, j, ALL, NP)
                if was:
                    if stacked(was[1]):
                        dve.wait_ge(s_lowv, n_kind(*was, "V") + 1)
                    else:
                        dve.wait_ge(s_mm, (n_tile if PLAN[was[1]] == "F" else n_late)(*was) + 1)
                if j in SQUARED:
                    u, nxt = j - N1, turn.shift(1)
                    if u == 0:
                        dve.wait_ge(s_thrice, nxt.count(1, 1))
                    dve.wait_ge(s_side, n_side(nxt, SQUARE_X + u) + 1)
                    nc.vector.tensor_tensor(to, side(nxt, SQUARE_X + u)[0:rows, :], x_thrice[0:rows, :],
                                            ALU.mult).then_inc(s_square, 1)
                    return
                t = j if j in PAIRED else j - N1 - N0
                if j in PAIRED:
                    if t == 0:
                        dve.wait_ge(s_z0, turn.count(1, 1))
                    dve.wait_ge(s_spread, turn.count(N1, t + 1))
                elif t == 0:
                    dve.wait_ge(s_z1, turn.count(1, 1))
                maps = maps1 if j in PAIRED else maps2
                nc.vector.tensor_tensor(to, spread[0:rows, t, :], maps[0:rows, :], ALU.mult).then_inc(s_prod, 1)

            def channel_sum(turn, which):
                src, ready, done = ((direct01, s_z1, s_sum01), (direct2, s_z2, s_sum2))[which]
                dve.wait_ge(ready, turn.count(1, 1))
                if not turn.odd and (not turn.fixed or turn.number() > 0):
                    dve.wait_ge(s_feat, turn.count(1, 0))
                nc.vector.tensor_reduce(sums[:, which, turn.odd, :],
                                        src[:, :].rearrange("p (d b) -> p b d", b=ROWS), AX.X, ALU.add
                                        ).then_inc(done, 1)

            def feature(turn, which):
                dve.wait_ge((s_sum01, s_sum2)[which], turn.count(1, 1))
                if which == 0 and (not turn.fixed or turn.number() > 1):
                    dve.wait_ge(s_kept, turn.group(16, 0))
                nc.vector.tensor_tensor(feat[:, which, :],
                                        sums[:, which, 0, :], sums[:, which, 1, :], ALU.add).then_inc(s_feat, 1)

            def emit(turn, j):
                nxt, last = turn.shift(1), turn.shift(-1)
                if has(turn, j):
                    product(turn, j)
                then, i = (turn, j - SUB) if j >= SUB else (last, j - SUB + TILES)
                if PLAN[i] == "V" and has(then, i):
                    low_part(then, i)
                if j == LOW_ROWS_AT and not turn.odd and turn.shift(2).real():
                    low_rows(turn.group(1, 2))
                if turn.real() and j == N1 + LZ + 2:
                    channel_sum(turn, 0)
                if turn.real() and turn.odd and j == N1 + LZ + 4:
                    feature(turn, 0)
                if turn.fixed and turn.number() == CHUNKS and j == SUB:
                    split_top()
                if last.real() and j == LZ + 2:
                    channel_sum(last, 1)
                if last.real() and last.odd and j == LZ + 4:
                    feature(last, 1)

            def split_top():
                nc.vector.memset(m_wc.bitcast(f32), 0.0)
                nc.vector.memset(m_ctx.bitcast(f32), 0.0).then_inc(s_gaps, 1)
                dve.wait_ge(s_gaps, 1)
                dve.wait_ge(s_mlp, 16 * MLP_LOADS)
                nc.vector.tensor_copy(m_w1h, m_w1)
                for place in (0, 64):
                    nc.vector.tensor_copy(m_wc[place:place + DENSE, :], m_w1d)
                nc.vector.tensor_copy(m_w2h, m_w2).then_inc(s_fold, 1)
                dve.wait_ge(s_fold, 4)
                nc.vector.tensor_tensor(m_wc[32:32 + DENSE, :], m_w1d, m_wc[0:DENSE, :], ALU.subtract)
                nc.vector.tensor_tensor(m_w1l, m_w1, m_w1h, ALU.subtract).then_inc(s_top, 1)
                nc.vector.tensor_tensor(m_w2l, m_w2, m_w2h, ALU.subtract).then_inc(s_top, 1)

            turns(dve, emit)

            def low_features(n):
                dve.wait_ge(s_fh, n + 1)
                part = slice(PER * n, PER * (n + 1))
                nc.vector.tensor_tensor(m_fl[:, part, :, :], m_feats[:, part, :, :], m_fh[:, part, :, :],
                                        ALU.subtract).then_inc(s_fl, 1)

            for i in range(2):
                dve.wait_ge(s_dense_c, i + 1)
                cols = slice(i * COLS, (i + 1) * COLS)
                nc.vector.tensor_tensor(m_ctx[64:CTX, cols], sides[i][0:DENSE, :], m_ctx[0:DENSE, cols],
                                        ALU.subtract).then_inc(s_ctx, 1)
            low_features(0)
            for n in range(4):
                for m in range(4):
                    dve.wait_ge(s_h1h, 4 * n + m + 1)
                    i = n % 2 * 4 + m
                    nc.vector.tensor_tensor(m_h1l[:, i, :], m_h1[:, i, :], m_h1h[:, i, :], ALU.subtract
                                            ).then_inc(s_h1l, 1)
                    if m == 0 and n < 3:
                        low_features(n + 1)

        @block.tensor
        def _(pe):
            def contract(turn, j):
                layer = layer_of(j)
                z = zacc[(turn.odd + {1: 0, 0: 1, 2: 0}[layer]) % 2]
                rows = rows_of(j)
                of = {1: PAIRED, 0: SQUARED, 2: LAST}[layer]
                first, last = j == of[0], j == of[-1] and tail(of) is None
                if first and layer == 1:
                    pe.wait_ge(s_z0, turn.count(1, 1))
                    if not turn.fixed or turn.number() > 0:
                        pe.wait_ge(s_z1, turn.count(1, 0))
                if first and layer == 0 and turn.real():
                    if not turn.fixed or turn.number() > 0:
                        pe.wait_ge(s_z2, turn.count(1, 0))
                if first and layer == 2:
                    pe.wait_ge(s_z1, turn.count(1, 1))

                def mm(hf, w, x, start, stop):
                    return nc.tensor.matmul(z[:, hf * BANK:(hf + 1) * BANK], w, x[:, hf * BANK:(hf + 1) * BANK],
                                            start=start, stop=stop)
                if PLAN[j] == "F":
                    if j in SQUARED:
                        pe.wait_ge(s_square, n_square(turn, j) + 1)
                    else:
                        pe.wait_ge(s_prod, n_prod(turn, j) + 1)
                    x = prod[0:rows, slot(j, ALL, NP), :]
                    for hf in range(2):
                        done = mm(hf, w_plain[0:rows, rank(j, "F"), :], x, first, last)
                else:
                    h, r = slot(j, "V", NH), rank(j, "V")
                    pe.wait_ge(s_round, n_kind(turn, j, "V") + 1)
                    for hf in range(2):
                        low_weights = mm(hf, w_low[0:rows, r, :], high[0:rows, h, :], first, False)
                    if stacked(j):
                        done = low_weights
                    else:
                        for hf in range(2):
                            done = mm(hf, w_high[0:rows, r, :], high[0:rows, h, :], False, False)
                return done

            def contract_low(turn, j):
                layer, rows = layer_of(j), rows_of(j)
                z = zacc[(turn.odd + {1: 0, 0: 1, 2: 0}[layer]) % 2]
                r = rank(j, "V")
                last = j == tail({1: PAIRED, 0: SQUARED, 2: LAST}[layer])
                pe.wait_ge(s_lowv, n_kind(turn, j, "V") + 1)
                x = low[0:rows, slot(j, ALL, NP), :]
                if stacked(j):
                    rows, x = 2 * HALF, high[:, slot(j, "V", NH), :]
                for hf in range(2):
                    cols = slice(hf * BANK, (hf + 1) * BANK)
                    done = nc.tensor.matmul(z[:, cols], w_high[0:rows, r, :], x[:, cols], start=False, stop=last)
                return done

            def side_work(turn, j):
                nxt = turn.shift(1)
                if not nxt.real():
                    return

                def pick_fields(use, first, n):
                    for hf in range(2):
                        cols = slice(hf * BANK, (hf + 1) * BANK)
                        done = nc.tensor.matmul(side(nxt, use)[0:n, cols], pick[:, first:first + n],
                                                x_split[:, cols], start=True, stop=True)
                    done.then_inc(s_side, 1)

                if j == TURN_AT:
                    pe.wait_ge(s_rows, nxt.group(1, 1))
                    if turn.real():
                        pe.wait_ge(s_spread, turn.count(N1, N1 - 1))
                    for d in range(CHAN):
                        done = nc.tensor.matmul(side(nxt, TURN_X)[0:SPLIT, d * ROWS:(d + 1) * ROWS],
                                                rows_split[:, nxt.odd * CHAN + d, :], ident_r[:, :],
                                                start=d * ROWS % BANK == 0, stop=(d + 1) * ROWS % BANK == 0,
                                                skip_group_check=True)
                    done.then_inc(s_side, 1)
                if j == THRICE_AT:
                    pe.wait_ge(s_x, nxt.count(1, 1))
                    if turn.real():
                        pe.wait_ge(s_spread, turn.count(N1, N1))
                    pick_fields(THRICE, BACK, TRIPLE)
                u = j - N1 + AHEAD
                if 0 <= u < N0:
                    if u == 1:
                        pe.wait_ge(s_thrice, nxt.count(1, 1))
                    elif u > 1:
                        pe.wait_ge(s_square, nxt.count(N0, u - 1))
                    pick_fields(SQUARE_X + u, PERIODIC + PER0 * u, TRIPLE)
                t = j - N1 - N0
                if 0 <= t:
                    if t < 2:
                        pe.wait_ge(s_square, nxt.count(N0, N0 - 1 + t))
                    else:
                        pe.wait_ge(s_spread, nxt.count(N1, t - 1))
                    pick_fields(SPREAD_X + t, t * MAPS, MAPS)

            def emit(turn, j):
                if turn.fixed and turn.number() == -1 and j == 0:
                    pe.wait_ge(s_pick, 1)
                if turn.fixed and turn.number() == -1 and j == N1:
                    pe.wait_ge(s_prep, 1)
                if has(turn, j):
                    done = contract(turn, j)
                    then = step_back(turn, j, LATE)
                    if then and PLAN[then[1]] == "V":
                        done = contract_low(*then)
                    done.then_inc(s_mm, 1)
                if turn.fixed and (turn.number(), j) in (
                        (-1, SQUARED[-1]), (CHUNKS - 1, PAIRED[-1]), (CHUNKS - 1, TILES - 1)):
                    for i in range(j - LATE + 1, j + 1):
                        if PLAN[i] == "V":
                            done = contract_low(turn, i)
                        else:
                            unused = zacc[1 if j in SQUARED else 0][0:2, 0:2]
                            done = nc.tensor.matmul(unused, ident_r[0:2, 0:2], ident_r[0:2, 0:2],
                                                    start=True, stop=True)
                        done.then_inc(s_mm, 1)
                side_work(turn, j)

            turns(pe, emit)

            pe.wait_ge(s_mlp, 16 * MLP_LOADS)
            for n in range(4):
                for g in range(PER):
                    done = nc.tensor.matmul(sides[n // 2][0:DENSE, n % 2 * BANK + g * ROWS:n % 2 * BANK + (g + 1) * ROWS],
                                            m_dense[:, PER * n + g, :], m_ident, start=g == 0, stop=g == PER - 1,
                                            skip_group_check=True)
                if n % 2:
                    done.then_inc(s_dense, 1)
            pe.wait_ge(s_z2, CHUNKS)
            pe.wait_ge(s_ctx, 2)
            for k, (layer, n, m) in enumerate(MLP_STEPS):
                if k >= 4:
                    pe.wait_ge(s_hc, k - 3)
                bank = mlp_bank(k)
                ms = slice(m * 128, (m + 1) * 128)
                if layer == 1:
                    if m == 0:
                        pe.wait_ge(s_fl, n + 1)
                    if k == 0:
                        pe.wait_ge(s_top, 1)
                    groups = slice(PER * n, PER * (n + 1))
                    nc.tensor.matmul(bank, m_wc[:, ms], m_ctx[:, n * BANK:(n + 1) * BANK], start=True, stop=False)
                    for w in range(2):
                        nc.tensor.matmul(bank, m_w1l[:, w, ms], m_fh[:, groups, w, :], start=False, stop=False)
                        nc.tensor.matmul(bank, m_w1h[:, w, ms], m_fh[:, groups, w, :], start=False, stop=False)
                        done = nc.tensor.matmul(bank, m_w1h[:, w, ms], m_fl[:, groups, w, :], start=False, stop=w == 1)
                elif layer == 2:
                    if n == m == 0:
                        pe.wait_ge(s_top, 2)
                    for q in range(4):
                        i = n % 2 * 4 + q
                        if m == 0:
                            pe.wait_ge(s_h1l, 4 * n + q + 1)
                        nc.tensor.matmul(bank, m_w2l[:, q, ms], m_h1h[:, i, :], start=q == 0, stop=False)
                        nc.tensor.matmul(bank, m_w2h[:, q, ms], m_h1h[:, i, :], start=False, stop=False)
                        done = nc.tensor.matmul(bank, m_w2h[:, q, ms], m_h1l[:, i, :], start=False, stop=q == 3)
                else:
                    pe.wait_ge(s_hc, MLP_STEPS.index((2, n, 1)) + 1)
                    for q in range(2):
                        done = nc.tensor.matmul(bank[0:1, :], m_w3[:, q:q + 1], m_h2[:, n % 2 * 2 + q, :],
                                                start=q == 0, stop=q == 1)
                done.then_inc(s_h, 1)


MLP_LOADS = 10
MLP_STEPS = [(layer, n, m) for layer, n in ((1, 0), (1, 1), (2, 0), (1, 2), (3, 0), (2, 1), (1, 3), (3, 1), (2, 2),
                                            (2, 3), (3, 2), (3, 3)) for m in range({1: 4, 2: 2, 3: 1}[layer])]


def w0_runs():
    runs = []
    for j in range(SHIFTS):
        u, s = divmod(j, PER0)
        cuts = sorted({0, s, FIELDS - PER0 * u, FIELDS})
        runs += [(u, s, lo, hi) for lo, hi in zip(cuts, cuts[1:])]
    return runs


W0_RUNS = w0_runs()
N_WLOADS = 2 * len(W0_RUNS) - sum(u == s == 0 for u, s, _, _ in W0_RUNS)


def selections():
    pick = np.zeros((SPLIT, PICK_W), np.float32)
    for at in (0, FIELDS):
        for f in range(FIELDS):
            pick[at + f, f * HALF:(f + 1) * HALF] = 1.0
            pick[at + f, PERIODIC + f:BACK:FIELDS] = 1.0
            for s in range(PER0):
                pick[at + f, BACK + s * FIELDS + (f + s) % FIELDS] = 1.0
    return pick


def kernel(**inputs):
    import concourse.bacc as _bacc
    from concourse.bass_utils import run_bass_kernel_spmd as _run

    nc = _bacc.Bacc("TRN2", target_bir_lowering=False, num_devices=1)
    arrays, args = {}, {}
    given = {name: np.ascontiguousarray(x) for name, x in inputs.items()}
    given["pick"] = selections()
    given["ident"] = np.eye(128, dtype=np.float32)
    for name, x in given.items():
        arrays[f"in_{name}"] = x
        args[name] = nc.dram_tensor(f"in_{name}", x.shape, mybir.dt.from_np(x.dtype), kind="ExternalInput").ap()
    out = nc.dram_tensor("out", (BATCH, 1), mybir.dt.float32, kind="ExternalOutput").ap()
    build(nc, args, out)
    return _run(nc, [arrays], core_ids=[0]).results[0]["out"]
```
